# Optimizing a Trainium2 kernel written in Bass

```python
import numpy as np
import jax
import jax.numpy as jnp

def _softmax(x, axis=-1):
    return jax.nn.softmax(x, axis=axis)

def _gelu(x):
    return jax.nn.gelu(x, approximate=True)

def _silu(x):
    return jax.nn.silu(x)

def _sigmoid(x):
    return jax.nn.sigmoid(x)

def _layernorm(x, axis=-1, eps=1e-05):
    m = jnp.mean(x, axis=axis, keepdims=True)
    v = jnp.var(x, axis=axis, keepdims=True)
    return (x - m) / jnp.sqrt(v + eps)

def _scatter_add(tgt, idx, src, axis=0):
    return tgt.at[idx].add(src)

def _segment_sum(src, seg, n):
    return jax.ops.segment_sum(src, seg, n)
kernel_name = 'mk_xattn_ffn_d1_seqx_r4_418a57'

def setup_inputs(seed: int=0):
    np.random.seed(seed)
    _w = jnp.asarray

    def _rec_inputs():
        import jax
        import jax.numpy as jnp
        _rk = jax.random.key(seed)
        x = -0.0003929 + 0.9999 * jax.random.normal(jax.random.fold_in(_rk, 1), (16, 256, 512), jnp.float32)
        _lenS = 256 - jax.random.randint(jax.random.fold_in(_rk, 7), (16,), 0, max(1, 256 // 4) + 1, jnp.int32)
        _lenS2 = 256 - jax.random.randint(jax.random.fold_in(_rk, 8), (16,), 0, max(1, 256 // 4) + 1, jnp.int32)
        _ctx_2048P = jax.random.normal(jax.random.fold_in(_rk, 11), (16, 16, 512), jnp.float32)
        _ctx_2048c = jax.random.dirichlet(jax.random.fold_in(_rk, 511), 0.3 * jnp.ones((16,), jnp.float32), (16, 256))
        _ctx_2048t = jnp.einsum('bsk,bkd->bsd', _ctx_2048c, _ctx_2048P)
        _ctx_2048t = _ctx_2048t * jax.lax.rsqrt(jnp.mean(jnp.square(_ctx_2048t)) + 1e-12) * 0.953939
        ctx_2048 = 2.81802e-05 + 1.00001 * (_ctx_2048t + 0.3 * jax.random.normal(jax.random.fold_in(_rk, 611), (16, 256, 512), jnp.float32))
        return (x, ctx_2048)
    x, ctx_2048 = _rec_inputs()

    def _L0_xattn_setup():
        import jax, jax.numpy as jnp
        import numpy as np
        HIDDEN = 512
        NUM_HEADS = 16
        HEAD_DIM = HIDDEN // NUM_HEADS
        CHUNK = 256
        SCALE = HEAD_DIM ** (-0.5)

        def _chunked_causal_attention(q, k, v):
            B, H, S, D = q.shape
            n_chunks = S // CHUNK
            kc = k.reshape(B, H, n_chunks, CHUNK, D).transpose(2, 0, 1, 3, 4)
            vc = v.reshape(B, H, n_chunks, CHUNK, D).transpose(2, 0, 1, 3, 4)
            j0s = jnp.arange(n_chunks) * CHUNK
            q_idx = jnp.arange(S)[:, None]
            k_off = jnp.arange(CHUNK)[None, :]
            out0 = jnp.zeros_like(q)
            m0 = jnp.full((B, H, S, 1), -jnp.inf, dtype=q.dtype)
            s0 = jnp.zeros((B, H, S, 1), dtype=q.dtype)

            def step(carry, inputs):
                out, m, s = carry
                kj, vj, j0 = inputs
                scores = jnp.einsum('bhqd,bhkd->bhqk', q, kj) * SCALE
                causal = j0 + k_off > q_idx
                scores = jnp.where(causal[None, None], -jnp.inf, scores)
                chunk_max = scores.max(axis=-1, keepdims=True)
                new_m = jnp.maximum(m, chunk_max)
                exp_old = jnp.exp(m - new_m)
                exp_c = jnp.exp(scores - new_m)
                new_s = s * exp_old + exp_c.sum(axis=-1, keepdims=True)
                out = out * (s / new_s) * exp_old + jnp.einsum('bhqk,bhkd->bhqd', exp_c / new_s, vj)
                return ((out, new_m, new_s), None)
            (out, _, _), _ = jax.lax.scan(step, (out0, m0, s0), (kc, vc, j0s))
            return out
        key = jax.random.key(seed)
        kq, kk, kv = jax.random.split(key, 3)
        B, S = (2, 1024)
        return {'query': jax.random.normal(kq, (B, S, HIDDEN), dtype=jnp.float32), 'key': jax.random.normal(kk, (B, S, HIDDEN), dtype=jnp.float32), 'value': jax.random.normal(kv, (B, S, HIDDEN), dtype=jnp.float32)}
    _L0_xattn_all = _L0_xattn_setup()
    _L0_xattn_in = {k: v for k, v in _L0_xattn_all.items() if k in ()}
    del _L0_xattn_all

    def _L0_ffn_setup():
        import jax, jax.numpy as jnp
        import numpy as np
        DIM_IN = 512
        DIM_HIDDEN = 2048
        key = jax.random.key(seed)
        k_x, k_g, k_u, k_d = jax.random.split(key, 4)
        s_in = 1.0 / np.sqrt(DIM_IN)
        s_hid = 1.0 / np.sqrt(DIM_HIDDEN)
        x = jax.random.normal(k_x, (4, 512, DIM_IN), dtype=jnp.float32)
        w_gate = jax.random.uniform(k_g, (DIM_HIDDEN, DIM_IN), jnp.float32, -s_in, s_in)
        w_up = jax.random.uniform(k_u, (DIM_HIDDEN, DIM_IN), jnp.float32, -s_in, s_in)
        w_down = jax.random.uniform(k_d, (DIM_IN, DIM_HIDDEN), jnp.float32, -s_hid, s_hid)
        return {'x': x, 'w_gate': w_gate, 'w_up': w_up, 'w_down': w_down}
    _L0_ffn_all = _L0_ffn_setup()
    _L0_ffn_in = {k: v for k, v in _L0_ffn_all.items() if k in ('w_gate', 'w_up', 'w_down')}
    del _L0_ffn_all
    return {'x': x, 'ctx_2048': ctx_2048, 'L0_ffn_w_gate': _L0_ffn_in['w_gate'], 'L0_ffn_w_up': _L0_ffn_in['w_up'], 'L0_ffn_w_down': _L0_ffn_in['w_down']}

def reference(x, ctx_2048, L0_ffn_w_gate, L0_ffn_w_up, L0_ffn_w_down):
    import jax
    import jax.numpy as jnp

    def _L0_xattn_ref(query, key, value):
        import jax, jax.numpy as jnp
        import numpy as np
        HIDDEN = 512
        NUM_HEADS = 16
        HEAD_DIM = HIDDEN // NUM_HEADS
        CHUNK = 256
        SCALE = HEAD_DIM ** (-0.5)

        def _chunked_causal_attention(q, k, v):
            B, H, S, D = q.shape
            n_chunks = S // CHUNK
            kc = k.reshape(B, H, n_chunks, CHUNK, D).transpose(2, 0, 1, 3, 4)
            vc = v.reshape(B, H, n_chunks, CHUNK, D).transpose(2, 0, 1, 3, 4)
            j0s = jnp.arange(n_chunks) * CHUNK
            q_idx = jnp.arange(S)[:, None]
            k_off = jnp.arange(CHUNK)[None, :]
            out0 = jnp.zeros_like(q)
            m0 = jnp.full((B, H, S, 1), -jnp.inf, dtype=q.dtype)
            s0 = jnp.zeros((B, H, S, 1), dtype=q.dtype)

            def step(carry, inputs):
                out, m, s = carry
                kj, vj, j0 = inputs
                scores = jnp.einsum('bhqd,bhkd->bhqk', q, kj) * SCALE
                causal = j0 + k_off > q_idx
                scores = jnp.where(causal[None, None], -jnp.inf, scores)
                chunk_max = scores.max(axis=-1, keepdims=True)
                new_m = jnp.maximum(m, chunk_max)
                exp_old = jnp.exp(m - new_m)
                exp_c = jnp.exp(scores - new_m)
                new_s = s * exp_old + exp_c.sum(axis=-1, keepdims=True)
                out = out * (s / new_s) * exp_old + jnp.einsum('bhqk,bhkd->bhqd', exp_c / new_s, vj)
                return ((out, new_m, new_s), None)
            (out, _, _), _ = jax.lax.scan(step, (out0, m0, s0), (kc, vc, j0s))
            return out
        B, S, _ = query.shape
        q = query.reshape(B, S, NUM_HEADS, HEAD_DIM).transpose(0, 2, 1, 3)
        k = key.reshape(B, S, NUM_HEADS, HEAD_DIM).transpose(0, 2, 1, 3)
        v = value.reshape(B, S, NUM_HEADS, HEAD_DIM).transpose(0, 2, 1, 3)
        out = _chunked_causal_attention(q, k, v)
        return out.transpose(0, 2, 1, 3).reshape(B, S, HIDDEN)

    def _L0_ffn_ref(x, w_gate, w_up, w_down):
        import jax, jax.numpy as jnp
        import numpy as np
        DIM_IN = 512
        DIM_HIDDEN = 2048
        gate = jnp.einsum('bsd,hd->bsh', x, w_gate)
        up = jnp.einsum('bsd,hd->bsh', x, w_up)
        gated = jax.nn.silu(gate) * up
        return jnp.einsum('bsh,dh->bsd', gated, w_down)
    x = x + _L0_xattn_ref(_layernorm(x, axis=-1), ctx_2048, ctx_2048)
    x = x + _L0_ffn_ref(_layernorm(x, axis=-1), L0_ffn_w_gate, L0_ffn_w_up, L0_ffn_w_down)
    return x

_drawn_inputs = setup_inputs


def setup_inputs(seed=0):
    import zlib

    import numpy as np

    out = dict(_drawn_inputs(seed))
    spreads = {}
    factors = {}
    for name, (base, spread) in spreads.items():
        noise = np.random.default_rng([zlib.crc32(name.encode()), seed]).standard_normal(out[name].shape)
        drawn = base * np.exp(spread * noise) if base else spread * noise
        out[name] = jnp.asarray(drawn.astype(out[name].dtype))
    for name, factor in factors.items():
        out[name] = (out[name] * factor).astype(out[name].dtype)
    return out
```

```python
from contextlib import ExitStack

import concourse.bass as bass
from concourse import mybir

F32 = mybir.dt.float32
F32R = mybir.dt.float32r
BF16 = mybir.dt.bfloat16
F16 = mybir.dt.float16
ALU = mybir.AluOpType
ACT = mybir.ActivationFunctionType
AX = mybir.AxisListType

P = 128
HEADS, HD = 16, 32
EPS = 1e-5
SCALE = HD ** -0.5
NEG = -3.0e38
P_SCALE = 2.0 ** 15
VP = HD + 1

T_PAIR = 4
H_PAIR = 2 * HEADS
FILLS = H_PAIR // 4
LAG_T, LAG_V = 1, 2
MM_TICK = 16
PARTS = ((0, 6), (6, 11), (11, 16))
STACK_INC = 16 * 12
USES = FILLS + T_PAIR

INPUT_NORM = {9: 1, 25: 2}
VALUES = {2: (0, 1), 12: (1, 0), 18: (1, 1), 28: (2, 0)}
Y_STATS = {(21, 2): 0, (33, 2): 1}
Y_NORM = {(33, 1): 0, (34, 1): 1, (34, 2): 2, (35, 1): 3}
Y_TURNED = {(34, 0): 0, (34, 1): 1, (35, 1): 2, (35, 2): 3}
Y_LO = {(34, 2): 0, (35, 0): 1, (35, 1): 2, (35, 2): 3}


def feed_forward_order(h_tiles, groups, kd):
    order = []
    per = h_tiles // groups
    for g in range(groups + 1):
        for i in range(per if g < groups else 0):
            j = g * per + i
            order += [("gate", j, 0, c) for c in range(3 * kd)]
            if i == 0 and g > 0:
                order += [("down", g - 1, t, c) for t in range(T_PAIR) for c in range(3 * per)]
            order += [("up", j, 0, c) for c in range(3 * kd)]
    order += [("down", groups - 1, t, c) for t in range(T_PAIR) for c in range(3 * per)]
    return order


def build(nc, x, ctx, gu_w, dn_w, out):
    batches, seq, dim = x.shape
    h_tiles = gu_w.shape[0]
    kd = dim // P
    groups = dn_w.shape[0]
    per = h_tiles // groups
    pairs = batches // 2
    assert seq == 2 * P and dim == HEADS * HD == 4 * P and batches % 2 == 0 and per == 2

    order = feed_forward_order(h_tiles, groups, kd)
    ticks = len(order) // MM_TICK
    assert ticks * MM_TICK == len(order) and ticks >= H_PAIR + LAG_V
    ends = {}
    for n, (kind, a, b, c) in enumerate(order):
        if c == (3 * kd if kind != "down" else 3 * per) - 1:
            part = next(i for i, (lo, hi) in enumerate(PARTS) if lo <= n % MM_TICK < hi)
            ends.setdefault((n // MM_TICK, part), []).append((kind, a, b))

    x_pair = x.rearrange("(i b) (t p) d -> i p (b t) d", b=2, p=P)
    out_pair = out.rearrange("(i b) (t p) d -> i p (b t) d", b=2, p=P)
    x_batch = x.rearrange("b (t p) d -> b p t d", p=P)
    ctx_batch = ctx.rearrange("b (t p) d -> b p t d", p=P)

    with ExitStack() as stack:
        def sb(name, shape, dt=F32):
            return stack.enter_context(nc.sbuf_tensor(name, shape, dt))

        def ps(name, shape=(P, 512), dt=F32):
            return stack.enter_context(nc.psum_tensor(name, list(shape), dt))

        def sem(name):
            return stack.enter_context(nc.semaphore(name))

        gu_hi = sb("gu_hi", [P, h_tiles, 2, kd, P], F32R)
        dn_hi = sb("dn_hi", [P, h_tiles, dim], F32R)
        gu_raw = sb("gu_raw", [P, 2, kd, P])
        dn_raw = sb("dn_raw", [P, per, dim])
        gu_lo = sb("gu_lo", [P, 2, 2, kd, P], F32R)
        dn_lo = sb("dn_lo", [P, per, dim], F32R)
        yt_hi = sb("yt_hi", [P, kd, T_PAIR * P], F32R)
        yt_lo = sb("yt_lo", [P, kd, T_PAIR * P], F32R)
        h_hi = sb("h_hi", [P, per, T_PAIR * P], F32R)
        h_lo = sb("h_lo", [P, per, T_PAIR * P], F32R)
        h_full = sb("h_full", [P, 2, T_PAIR * P])
        x_ffn = sb("x_ffn", [P, T_PAIR, dim])
        x_att = sb("x_att", [P, T_PAIR, dim])
        x_in = sb("x_in", [P, 2, dim])
        ctx_in = sb("ctx_in", [P, 2, dim])
        split = sb("split", [P, 4, 2 * P], F32R)
        stacks = sb("stacks", [P, 2, 4, 2, 2 * P], F32R)
        v_parts = sb("v_parts", [P, 2, HEADS, 3, VP], BF16)
        v_rest = sb("v_rest", [P, 2, HEADS // 2, HD])
        probs = sb("probs", [P, 2, 3 * P])
        pt_hi = sb("pt_hi", [P, 2, 3 * P], F16)
        pt_lo = sb("pt_lo", [P, 2, 3 * P], F16)
        heads_out = sb("heads_out", [P, 2, 4, VP])
        quotient = sb("quotient", [P, 2, 4])
        y_in = sb("y_in", [P, dim])
        neg_max = sb("neg_max", [P, 2, 2])
        in_stats, y_stats = sb("in_stats", [P, 2, 6]), sb("y_stats", [P, 2, 6])
        in_moments, y_moments = sb("in_moments", [P, 2, 2]), sb("y_moments", [P, T_PAIR, 2])
        in_var, y_var = sb("in_var", [P, 2]), sb("y_var", [P, T_PAIR])
        in_rstd, y_rstd = sb("in_rstd", [P, 2]), sb("y_rstd", [P, T_PAIR])
        minus_half = sb("minus_half", [P, 2])
        mask = sb("mask", [P, 2 * P])
        ident = sb("ident", [P, P])

        gate_ps, up_ps = ps("gate_ps"), ps("up_ps")
        down_ps = [ps("down_ps0"), ps("down_ps1")]
        score_ps, pt_ps, pv_ps, turn_ps = ps("score_ps"), ps("pt_ps"), ps("pv_ps"), ps("turn_ps")

        x_in_loaded, ctx_loaded, x_att_loaded = sem("x_in_loaded"), sem("ctx_loaded"), sem("x_att_loaded")
        x_ffn_loaded, out_stored = sem("x_ffn_loaded"), sem("out_stored")
        gu_loaded, dn_loaded = sem("gu_loaded"), sem("dn_loaded")
        stack_loaded = [sem("stack_loaded0"), sem("stack_loaded1")]
        scores_done, pt_done, pv_done, turned = sem("scores_done"), sem("pt_done"), sem("pv_done"), sem("turned")
        gate_done, up_done, down_done = sem("gate_done"), sem("up_done"), sem("down_done")
        masked, pt_lo_done, pv_reduced = sem("masked"), sem("pt_lo_done"), sem("pv_reduced")
        quotient_done, heads_scaled, x_att_added = sem("quotient_done"), sem("heads_scaled"), sem("x_att_added")
        in_stats_done, in_moments_done, in_var_done, in_normed = (
            sem("in_stats_done"), sem("in_moments_done"), sem("in_var_done"), sem("in_normed"))
        y_stats_done, y_moments_done, y_var_done, y_normed = (
            sem("y_stats_done"), sem("y_moments_done"), sem("y_var_done"), sem("y_normed"))
        turn_lo_done = sem("turn_lo_done")
        gate_free, up_free, down_free = sem("gate_free"), sem("up_free"), sem("down_free")
        exp_done, pt_hi_done, turn_hi_done = sem("exp_done"), sem("pt_hi_done"), sem("turn_hi_done")
        tanh_done, h_hi_done = sem("tanh_done"), sem("h_hi_done")
        v1_done, v2_done, gu_hi_done, dn_hi_done = sem("v1_done"), sem("v2_done"), sem("gu_hi_done"), sem("dn_hi_done")
        zeroed, consts_ready = sem("zeroed"), sem("consts_ready")
        in_rstd_done, y_rstd_done = sem("in_rstd_done"), sem("y_rstd_done")
        v_rest_done, v_ready = sem("v_rest_done"), sem("v_ready")
        h_lo_done, gu_lo_done, dn_lo_done = sem("h_lo_done"), sem("gu_lo_done"), sem("dn_lo_done")

        sp_passed, dve_passed = sem("sp_passed"), sem("dve_passed")

        block = stack.enter_context(nc.Block())


        def starts(i, k=0):
            return isinstance(i, int) and i == 0 and k == 0

        def row(array, i):
            if isinstance(i, int):
                return array[i]
            names = "abcd"[:len(array.shape) - 1]
            return array[bass.ds(i, 1)].rearrange(f"z {' '.join(names)} -> (z a) {' '.join(names[1:])}")

        def fill_at(t, more):
            return t // 4 + 1 if t % 4 == 0 and t < (H_PAIR if more else H_PAIR - 4) else None

        def fill_use(i, g):
            return USES * i + g

        def y_use(i, tile, more):
            return USES * i + (FILLS + 1 if more else FILLS) + tile

        def gates_ended(t, part):
            before = (t, part - 1) if part else (t - 1, 2)
            return [a for kind, a, _ in ends.get(before, []) if kind == "gate"]

        @block.sync
        def _(sp):
            def load_batch(i, b):
                n = 2 * i + b
                if not starts(i, b):
                    sp.wait_ge(turned, USES * i + 4 * b)
                    sp.sem_inc(sp_passed, 1)
                    sp.wait_ge(v_ready, 2 * n)
                    sp.sem_inc(sp_passed, 1)
                sp.dma_start(x_in[:], row(x_batch, n)).then_inc(x_in_loaded, 16)
                sp.dma_start(ctx_in[:], row(ctx_batch, n)).then_inc(ctx_loaded, 16)

            def fill_stack(i, g):
                sp.wait_ge(turn_lo_done, fill_use(i, g) + 1)
                sp.sem_inc(sp_passed, 1)
                if not (isinstance(i, int) and FILLS * i + g < 2):
                    sp.wait_ge(scores_done, H_PAIR * i + 4 * (g - 1))
                for r, parts in enumerate((slice(0, 3, 2), slice(0, 4, 3), slice(1, 3, 1))):
                    for j in range(4):
                        sp.dma_start(stacks[HD * r:HD * r + HD, g % 2, j, :, :].bitcast(F32),
                                     split[HD * j:HD * j + HD, parts, :].bitcast(F32)).then_inc(stack_loaded[g % 2], 16)

            def load_gu(j):
                sp.dma_start(gu_raw[:], gu_w[j]).then_inc(gu_loaded, 16)

            def load_dn(k):
                sp.dma_start(dn_raw[:], dn_w[k]).then_inc(dn_loaded, 16)

            def hand_over(i):
                sp.wait_ge(y_normed, T_PAIR * i)
                sp.dma_start(x_ffn[:], x_att[:]).then_inc(x_ffn_loaded, 16)

            def load_pair(i):
                if not starts(i):
                    sp.wait_ge(x_ffn_loaded, 16 * i)
                    sp.sem_inc(sp_passed, 1)
                sp.dma_start(x_att[:], row(x_pair, i)).then_inc(x_att_loaded, 16)

            def attention(i, t, more):
                if fill_at(t, more) is not None:
                    fill_stack(i, fill_at(t, more))
                if t == 8:
                    load_batch(i, 1)
                if t == 24 and more:
                    load_batch(i, 2)

            def feed_forward(i, t, last):
                for part in range(3):
                    for kind, a, b in ends.get((t, part), []):
                        if kind == "up" and not (last and a + 3 >= h_tiles):
                            sp.wait_ge(gu_lo_done, h_tiles * (i - 1) + a + 3)
                            load_gu((a + 3) % h_tiles)
                        if kind == "down" and b == T_PAIR - 1 and not (last and a + 2 >= groups):
                            sp.wait_ge(dn_lo_done, groups * (i - 1) + a + 2)
                            load_dn((a + 2) % groups)

            def store(i):
                for tile in range(T_PAIR):
                    sp.wait_ge(down_free, 2 + groups * T_PAIR * i - T_PAIR + tile + 1)
                    sp.sem_inc(sp_passed, 1)
                    sp.dma_start(row(out_pair, i - 1)[:, tile, :], x_ffn[:, tile, :]).then_inc(out_stored, 16)
                sp.wait_ge(out_stored, 16 * T_PAIR * i)
                sp.sem_inc(sp_passed, 1)

            load_batch(0, 0)
            load_gu(0)
            load_dn(0)
            load_pair(0)
            fill_stack(0, 0)
            for t in range(ticks):
                attention(0, t, True)
                if t + 1 < h_tiles + 3:
                    if t + 1 <= h_tiles:
                        sp.wait_ge(gu_hi_done, t + 1)
                    else:
                        sp.wait_ge(gu_lo_done, t + 1 - h_tiles)
                    load_gu((t + 1) % h_tiles)
                if t % 2 == 1 and t // 2 + 1 < groups + 2:
                    if t // 2 + 1 <= groups:
                        sp.wait_ge(dn_hi_done, t // 2 + 1)
                    else:
                        sp.wait_ge(dn_lo_done, t // 2 + 1 - groups)
                    load_dn((t // 2 + 1) % groups)

            def pair(i, more):
                hand_over(i)
                load_pair(i)
                for t in range(ticks):
                    attention(i, t, more)
                    feed_forward(i, t, False)
                store(i)

            with sp.Fori(1, pairs - 1) as i:
                pair(i, True)
            pair(pairs - 1, False)
            hand_over(pairs)
            for t in range(ticks):
                feed_forward(pairs, t, True)
            store(pairs)

        @block.tensor
        def _(pe):
            def turn_qk(i, g):
                if g % 4 == 0:
                    pe.wait_ge(in_normed, 2 * (2 * i + g // 4) + 2)
                    pe.wait_ge(ctx_loaded, 16 * (2 * i + g // 4) + 16)
                if not starts(i, g):
                    pe.wait_ge(turn_lo_done, fill_use(i, g))
                c = (g % 4) * P
                for n, source in enumerate((x_in, ctx_in)):
                    for tile in range(2):
                        mm = pe.transpose(turn_ps[:, (2 * n + tile) * P:(2 * n + tile + 1) * P],
                                          source[:, tile, c:c + P], ident[:])
                mm.then_inc(turned, 1)

            def scores(i, t):
                if t % 4 == 0:
                    pe.wait_ge(stack_loaded[t // 4 % 2], STACK_INC * (FILLS // 2 * i + t // 8 + 1))
                if not starts(i, t):
                    pe.wait_ge(masked, 2 * (H_PAIR * i + t))
                s = stacks[0:3 * HD, t // 4 % 2, t % 4]
                for tile in range(2):
                    mm = pe.matmul(score_ps[:, tile * 2 * P:(tile + 1) * 2 * P],
                                   s[:, 0, tile * P:(tile + 1) * P], s[:, 1, :], start=True, stop=True)
                mm.then_inc(scores_done, 1)

            def turn_probs(i, t):
                pe.wait_ge(exp_done, 2 * (H_PAIR * i + t) + 2)
                if not starts(i, t):
                    pe.wait_ge(pt_lo_done, H_PAIR * i + t)
                for n in range(3):
                    mm = pe.transpose(pt_ps[:, n * P:(n + 1) * P], probs[:, t % 2, n * P:(n + 1) * P], ident[:])
                mm.then_inc(pt_done, 1)

            def values(i, t):
                if t % 8 == 0:
                    pe.wait_ge(v_ready, 4 * i + t // 8 + 1)
                pe.wait_ge(pt_lo_done, H_PAIR * i + t + 1)
                if not starts(i, t):
                    pe.wait_ge(pv_reduced, H_PAIR * i + t)
                for tile, blocks in enumerate((((0, 0),), ((1, 0), (2, 1)))):
                    for n, (b, keys) in enumerate(blocks):
                        for part in (pt_hi, pt_lo):
                            mm = pe.matmul(pv_ps[:, tile * 3 * VP:(tile + 1) * 3 * VP],
                                           part[:, t % 2, b * P:(b + 1) * P],
                                           v_parts[:, keys, t % HEADS].rearrange("p a v -> p (a v)"),
                                           start=(n == 0 and part is pt_hi),
                                           stop=(n == len(blocks) - 1 and part is pt_lo))
                mm.then_inc(pv_done, 1)

            def turn_y(i, tile, more):
                pe.wait_ge(y_normed, T_PAIR * i + tile + 1)
                if tile != 1:
                    pe.wait_ge(turn_lo_done, y_use(i, tile, more) - (1 if tile else 0))
                for k in range(kd):
                    mm = pe.transpose((turn_ps, score_ps)[tile % 2][:, k * P:(k + 1) * P],
                                      y_in[:, k * P:(k + 1) * P], ident[:])
                mm.then_inc(turned, 1)

            def product(i, n):
                kind, a, b, c = order[n]
                if kind == "down":
                    hh, term = divmod(c, 3)
                    if c == 0:
                        pe.wait_ge(down_free, groups * T_PAIR * (i - 1) + a * T_PAIR + b + 1)
                    if b == 0 and c == 0:
                        pe.wait_ge(dn_lo_done, groups * (i - 1) + a + 1)
                    if b == 0 and term == 0:
                        pe.wait_ge(h_lo_done, 2 + h_tiles * (i - 1) + per * a + hh + 1)
                    mm = pe.matmul(down_ps[b % 2][:], (h_lo if term == 1 else h_hi)[:, hh, b * P:(b + 1) * P],
                                   dn_lo[:, hh] if term == 2 else dn_hi[:, per * a + hh],
                                   start=(c == 0), stop=(c == 3 * per - 1))
                    if c == 3 * per - 1:
                        mm.then_inc(down_done, 1)
                    return
                u = 0 if kind == "gate" else 1
                k, term = divmod(c, 3)
                if c == 0:
                    pe.wait_ge((gate_free, up_free)[u], h_tiles * (i - 1) + a + 1)
                if c == 0 and u == 0:
                    pe.wait_ge(gu_lo_done, h_tiles * (i - 1) + a + 1)
                mm = pe.matmul((gate_ps, up_ps)[u][:],
                               gu_lo[:, a % 2, u, k] if term == 2 else gu_hi[:, a, u, k],
                               (yt_lo if term == 1 else yt_hi)[:, k, :], start=(c == 0), stop=(c == 3 * kd - 1))
                if c == 3 * kd - 1:
                    mm.then_inc((gate_done, up_done)[u], 1)

            def pair(i, attend=True, feed=True, more=True):
                if feed:
                    pe.wait_ge(turn_lo_done, USES * i + (1 if attend else 0))
                for t in range(ticks):
                    for part, (lo, hi) in enumerate(PARTS):
                        if attend and part == 0 and t < H_PAIR:
                            scores(i, t)
                        if attend and part == 0 and fill_at(t, more) is not None:
                            turn_qk(i, fill_at(t, more))
                        if attend and part == 1 and 0 <= t - LAG_T < H_PAIR:
                            turn_probs(i, t - LAG_T)
                        if attend and part == 2 and 0 <= t - LAG_V < H_PAIR:
                            values(i, t - LAG_V)
                        if attend and (t, part) in Y_TURNED:
                            turn_y(i, Y_TURNED[t, part], more)
                        if feed:
                            for n in range(MM_TICK * t + lo, MM_TICK * t + hi):
                                product(i, n)

            pe.wait_ge(consts_ready, 3)
            turn_qk(0, 0)
            pair(0, feed=False)
            pe.wait_ge(gu_hi_done, h_tiles)
            pe.wait_ge(dn_hi_done, groups)
            with pe.Fori(1, pairs - 1) as i:
                pair(i)
            pair(pairs - 1, more=False)
            pair(pairs, attend=False)

        @block.vector
        def _(dve):
            def input_norm(i, b):
                n = 2 * i + b
                dve.wait_ge(x_in_loaded, 16 * n + 16)
                for tile in range(2):
                    dve.bn_stats(in_stats[:, tile, :], x_in[:, tile, :]).then_inc(in_stats_done, 1)
                dve.wait_ge(in_stats_done, 2 * n + 2)
                dve.sem_inc(dve_passed, 1)
                for tile in range(2):
                    dve.bn_aggr(in_moments[:, tile, :], in_stats[:, tile, :]).then_inc(in_moments_done, 1)
                dve.wait_ge(in_moments_done, 2 * n + 2)
                dve.tensor_scalar(in_var[:], in_moments[:, :, 1], EPS, None, ALU.add).then_inc(in_var_done, 1)
                dve.wait_ge(in_rstd_done, n + 1)
                for tile in range(2):
                    dve.tensor_scalar(x_in[:, tile, :], x_in[:, tile, :], in_moments[:, tile, 0:1],
                                      in_rstd[:, tile:tile + 1], ALU.subtract, ALU.mult).then_inc(in_normed, 1)

            def y_stats_of(i, half):
                dve.wait_ge(x_att_added, FILLS * i + 4 * half + 4)
                for tile in range(2):
                    dve.bn_stats(y_stats[:, tile, :], x_att[:, 2 * half + tile, :]).then_inc(y_stats_done, 1)
                dve.wait_ge(y_stats_done, 4 * i + 2 * half + 2)
                dve.sem_inc(dve_passed, 1)
                for tile in range(2):
                    dve.bn_aggr(y_moments[:, 2 * half + tile, :], y_stats[:, tile, :]).then_inc(y_moments_done, 1)
                dve.wait_ge(y_moments_done, 4 * i + 2 * half + 2)
                dve.tensor_scalar(y_var[:, 2 * half:2 * half + 2], y_moments[:, 2 * half:2 * half + 2, 1], EPS, None, ALU.add).then_inc(y_var_done, 1)

            def y_norm(i, tile, more):
                if tile % 2 == 0:
                    dve.wait_ge(y_rstd_done, 2 * i + tile // 2 + 1)
                if tile:
                    dve.wait_ge(turned, y_use(i, tile, more))
                dve.tensor_scalar(y_in[:], x_att[:, tile, :], y_moments[:, tile, 0:1],
                                  y_rstd[:, tile:tile + 1], ALU.subtract, ALU.mult).then_inc(y_normed, 1)

            def mask_scores(i, t):
                dve.wait_ge(scores_done, H_PAIR * i + t + 1)
                if not (isinstance(i, int) and H_PAIR * i + t < 2):
                    dve.wait_ge(pt_done, H_PAIR * i + t - 1)
                dve.sem_inc(dve_passed, 1)
                for tile, (lo, hi, m) in enumerate(((0, P, P), (P, 3 * P, 0))):
                    dve.tensor_tensor_reduce(probs[:, t % 2, lo:hi], score_ps[:, tile * 2 * P:tile * 2 * P + hi - lo],
                                             mask[:, m:], -SCALE, -NEG, ALU.add, ALU.min,
                                             neg_max[:, t % 2, tile:tile + 1]).then_inc(masked, 1)

            def split_qk_lo(i, g):
                use = fill_use(i, g)
                dve.wait_ge(turn_hi_done, use + 1)
                dve.tensor_tensor(split[:, 1:4:2, :], turn_ps[:].rearrange("p (a n) -> p a n", a=2),
                                  split[:, 0:4:2, :].bitcast(F32), ALU.subtract).then_inc(turn_lo_done, 1)

            def split_y_lo(i, tile, more):
                dve.wait_ge(turn_hi_done, y_use(i, tile, more) + 1)
                cols = slice(tile * P, (tile + 1) * P)
                dve.tensor_tensor(yt_lo[:, :, cols], (turn_ps, score_ps)[tile % 2][:].rearrange("p (k n) -> p k n", k=kd),
                                  yt_hi[:, :, cols].bitcast(F32), ALU.subtract).then_inc(turn_lo_done, 1)

            def split_probs_lo(i, t):
                dve.wait_ge(pt_hi_done, H_PAIR * i + t + 1)
                dve.scalar_tensor_tensor(out=pt_lo[:, t % 2, :], in0=pt_ps[:, 0:3 * P], scalar=P_SCALE,
                                         in1=pt_hi[:, t % 2, :], op0=ALU.mult, op1=ALU.subtract
                                         ).then_inc(pt_lo_done, 1)

            def collect_head(i, t):
                dve.wait_ge(pv_done, H_PAIR * i + t + 1)
                if t % 4 == 0 and not starts(i, t):
                    dve.wait_ge(x_att_added, FILLS * i + t // 4)
                dve.tensor_reduce(heads_out[:, :, t % 4, :],
                                  pv_ps[:, 0:6 * VP].rearrange("p (q a v) -> p q v a", q=2, a=3),
                                  AX.X, ALU.add).then_inc(pv_reduced, 1)
                if t % 4 < 3:
                    return
                g = t // 4
                dve.wait_ge(pv_reduced, H_PAIR * i + t + 1)
                dve.reciprocal(quotient[:], heads_out[:, :, :, HD]).then_inc(quotient_done, 1)
                dve.wait_ge(quotient_done, FILLS * i + g + 1)
                dve.tensor_tensor(heads_out[:, :, :, 0:HD], heads_out[:, :, :, 0:HD],
                                  quotient[:].unsqueeze(3).broadcast_to([P, 2, 4, HD]), ALU.mult
                                  ).then_inc(heads_scaled, 1)
                if g == 0:
                    dve.wait_ge(x_att_loaded, 16 * i + 16)
                dve.wait_ge(heads_scaled, FILLS * i + g + 1)
                xs = x_att[:, 2 * (g // 4):2 * (g // 4) + 2, (g % 4) * P:(g % 4 + 1) * P].rearrange(
                    "p q (h d) -> p q h d", h=4)
                dve.tensor_tensor(xs, xs, heads_out[:, :, :, 0:HD], ALU.add).then_inc(x_att_added, 1)

            def gated(i, j):
                n = h_tiles * (i - 1) + j
                dve.wait_ge(tanh_done, n + 1)
                hf = h_full[:, j % 2, :]
                dve.scalar_tensor_tensor(out=hf, in0=hf, scalar=1.0, in1=gate_ps[:], op0=ALU.add, op1=ALU.mult
                                         ).then_inc(gate_free, 1)

            def hidden(i, j):
                n = h_tiles * (i - 1) + j
                dve.wait_ge(up_done, n + 1)
                dve.wait_ge(gate_free, n + 2)
                hf = h_full[:, j % 2, :]
                dve.scalar_tensor_tensor(out=hf, in0=hf, scalar=0.5, in1=up_ps[:], op0=ALU.mult, op1=ALU.mult
                                         ).then_inc(up_free, 1)

            def add_down(i, k, tile):
                n = groups * T_PAIR * (i - 1) + T_PAIR * k + tile
                dve.wait_ge(down_done, n + 1)
                if k == 0 and tile == 0:
                    dve.wait_ge(x_ffn_loaded, 16 * i)
                if k:
                    dve.wait_ge(down_free, 2 + n - T_PAIR + 1)
                dve.tensor_tensor(x_ffn[:, tile, :], x_ffn[:, tile, :], down_ps[tile % 2][:], ALU.add
                                  ).then_inc(down_free, 1)

            def pair(i, attend=True, feed=True, more=True):
                for t in range(ticks):
                    for part in range(3):
                        if attend and part == 0 and t < H_PAIR:
                            mask_scores(i, t)
                        if attend and part == 1 and fill_at(t, more) is not None:
                            split_qk_lo(i, fill_at(t, more))
                        if attend and part == 1 and 0 <= t - LAG_T < H_PAIR:
                            split_probs_lo(i, t - LAG_T)
                        if attend and part == 2 and 0 <= t - LAG_V < H_PAIR:
                            collect_head(i, t - LAG_V)
                        if attend and part == 2 and t in INPUT_NORM and (more or INPUT_NORM[t] == 1):
                            input_norm(i, INPUT_NORM[t])
                        if attend and (t, part) in Y_STATS:
                            y_stats_of(i, Y_STATS[t, part])
                        if attend and (t, part) in Y_NORM:
                            y_norm(i, Y_NORM[t, part], more)
                        if feed:
                            for j in gates_ended(t, part):
                                gated(i, j)
                            for kind, a, b in ends.get((t, part), []):
                                if kind == "up":
                                    hidden(i, a)
                                if kind == "down":
                                    add_down(i, a, b)
                        if attend and (t, part) in Y_LO:
                            split_y_lo(i, Y_LO[t, part], more)

            dve.sem_inc(gate_free, 1)
            dve.sem_inc(up_free, 1)
            dve.sem_inc(down_free, 2)
            dve.wait_ge(consts_ready, 3)
            input_norm(0, 0)
            split_qk_lo(0, 0)
            pair(0, feed=False)
            with dve.Fori(1, pairs - 1) as i:
                pair(i)
            pair(pairs - 1, more=False)
            pair(pairs, attend=False)

        @block.scalar
        def _(act):
            def exponentials(i, t):
                for tile, (lo, hi) in enumerate(((0, P), (P, 3 * P))):
                    act.wait_ge(masked, 2 * (H_PAIR * i + t) + tile + 1)
                    p = probs[:, t % 2, lo:hi]
                    act.activation(p, p, ACT.Exp, bias=neg_max[:, t % 2, tile:tile + 1], scale=-1.0
                                   ).then_inc(exp_done, 1)

            def split_qk_hi(i, g):
                act.wait_ge(turned, fill_use(i, g) + 1)
                if not starts(i, g):
                    act.wait_ge(stack_loaded[(g - 1) % 2], STACK_INC * (FILLS // 2 * i + (g - 1) // 2 + 1))
                act.activation(split[:, 0:4:2, :], turn_ps[:].rearrange("p (a n) -> p a n", a=2), ACT.Copy
                               ).then_inc(turn_hi_done, 1)

            def split_y_hi(i, tile, more):
                act.wait_ge(turned, y_use(i, tile, more) + 1)
                if tile == 0 and not starts(i):
                    act.wait_ge(up_done, h_tiles * i)
                act.activation(yt_hi[:, :, tile * P:(tile + 1) * P],
                               (turn_ps, score_ps)[tile % 2][:].rearrange("p (k n) -> p k n", k=kd), ACT.Copy
                               ).then_inc(turn_hi_done, 1)

            def split_probs_hi(i, t):
                act.wait_ge(pt_done, H_PAIR * i + t + 1)
                if not (isinstance(i, int) and H_PAIR * i + t < 2):
                    act.wait_ge(pv_done, H_PAIR * i + t - 1)
                act.activation(pt_hi[:, t % 2, :], pt_ps[:, 0:3 * P], ACT.Copy, scale=P_SCALE
                               ).then_inc(pt_hi_done, 1)

            def values_first(i, b, half):
                n = 2 * i + b
                act.wait_ge(ctx_loaded, 16 * n + 16)
                if not starts(i, b):
                    act.wait_ge(pv_done, HEADS * n - HEADS // 2 + 8 * half)
                h = slice(8 * half, 8 * half + 8)
                act.activation(v_parts[:, :, h, 0, 0:HD],
                               ctx_in[:].rearrange("p t (h d) -> p t h d", h=HEADS)[:, :, h, :], ACT.Copy
                               ).then_inc(v1_done, 1)

            def values_second(i, b, half):
                act.wait_ge(v_rest_done, 2 * (2 * i + b) + half + 1)
                act.activation(v_parts[:, :, 8 * half:8 * half + 8, 1, 0:HD], v_rest[:], ACT.Copy
                               ).then_inc(v2_done, 1)

            def tanh(i, j):
                n = h_tiles * (i - 1) + j
                act.wait_ge(gate_done, n + 1)
                act.wait_ge(h_lo_done, n + 1)
                act.activation(h_full[:, j % 2, :], gate_ps[:], ACT.Tanh, scale=0.5).then_inc(tanh_done, 1)

            def split_h_hi(i, j):
                act.wait_ge(up_free, h_tiles * (i - 1) + j + 2)
                act.activation(h_hi[:, j % per, :], h_full[:, j % 2, :], ACT.Copy).then_inc(h_hi_done, 1)

            def weights_hi(t):
                if t < h_tiles:
                    act.wait_ge(gu_loaded, 16 * t + 16)
                    act.activation(gu_hi[:, t], gu_raw[:], ACT.Copy).then_inc(gu_hi_done, 1)
                if t % 2 == 0 and t // 2 < groups:
                    act.wait_ge(dn_loaded, 16 * (t // 2) + 16)
                    act.activation(dn_hi[:, t // 2 * per:(t // 2 + 1) * per], dn_raw[:], ACT.Copy
                                   ).then_inc(dn_hi_done, 1)

            def pair(i, attend=True, feed=True, more=True, load=False):
                for t in range(ticks):
                    for part in range(3):
                        if attend and part == 0 and t < H_PAIR:
                            exponentials(i, t)
                        if attend and part == 0 and fill_at(t, more) is not None:
                            split_qk_hi(i, fill_at(t, more))
                        if attend and part == 1 and 0 <= t - LAG_T < H_PAIR:
                            split_probs_hi(i, t - LAG_T)
                        if attend and part == 1 and t in VALUES and (more or VALUES[t][0] < 2):
                            values_first(i, *VALUES[t])
                        if attend and part == 2 and t in VALUES and (more or VALUES[t][0] < 2):
                            values_second(i, *VALUES[t])
                        if feed:
                            for kind, a, b in ends.get((t, part), []):
                                if kind == "gate":
                                    tanh(i, a)
                                if kind == "up":
                                    split_h_hi(i, a)
                        if attend and (t, part) in Y_LO:
                            split_y_hi(i, Y_LO[t, part], more)
                        if load and part == 2:
                            weights_hi(t)

            act.wait_ge(consts_ready, 3)
            values_first(0, 0, 0)
            split_qk_hi(0, 0)
            values_second(0, 0, 0)
            pair(0, feed=False, load=True)
            with act.Fori(1, pairs - 1) as i:
                pair(i)
            pair(pairs - 1, more=False)
            pair(pairs, attend=False)

        @block.gpsimd
        def _(pool):
            def input_rstd(i, b):
                pool.wait_ge(in_var_done, 2 * i + b + 1)
                pool.tensor_tensor(in_rstd[:], in_var[:], minus_half[:], ALU.pow).then_inc(in_rstd_done, 1)

            def y_rstd_of(i, half):
                pool.wait_ge(y_var_done, 2 * i + half + 1)
                pool.tensor_tensor(y_rstd[:, 2 * half:2 * half + 2], y_var[:, 2 * half:2 * half + 2], minus_half[:], ALU.pow).then_inc(y_rstd_done, 1)

            def values_rest(i, b, half):
                h = slice(8 * half, 8 * half + 8)
                pool.wait_ge(v1_done, 2 * (2 * i + b) + half + 1)
                if not starts(i, 2 * b + half):
                    pool.wait_ge(v_ready, 2 * (2 * i + b) + half)
                pool.tensor_tensor(v_rest[:], ctx_in[:].rearrange("p t (h d) -> p t h d", h=HEADS)[:, :, h, :],
                                   v_parts[:, :, h, 0, 0:HD], ALU.subtract).then_inc(v_rest_done, 1)

            def values_third(i, b, half):
                pool.wait_ge(v2_done, 2 * (2 * i + b) + half + 1)
                h = slice(8 * half, 8 * half + 8)
                pool.tensor_tensor(v_parts[:, :, h, 2, 0:HD], v_rest[:], v_parts[:, :, h, 1, 0:HD],
                                   ALU.subtract).then_inc(v_ready, 1)

            def split_h_lo(i, j):
                pool.wait_ge(h_hi_done, h_tiles * (i - 1) + j + 1)
                pool.tensor_tensor(h_lo[:, j % per, :], h_full[:, j % 2, :], h_hi[:, j % per, :].bitcast(F32),
                                   ALU.subtract).then_inc(h_lo_done, 1)

            def weights_gu_lo(n, j):
                pool.wait_ge(gu_loaded, 16 * (h_tiles + n + 1))
                pool.tensor_tensor(gu_lo[:, j % 2].rearrange("p u k n -> p (u k n)"),
                                   gu_raw[:].rearrange("p u k n -> p (u k n)"),
                                   gu_hi[:, j].bitcast(F32).rearrange("p u k n -> p (u k n)"), ALU.subtract
                                   ).then_inc(gu_lo_done, 1)

            def weights_dn_lo(n, k):
                pool.wait_ge(dn_loaded, 16 * (groups + n + 1))
                pool.tensor_tensor(dn_lo[:], dn_raw[:], dn_hi[:, per * k:per * (k + 1)].bitcast(F32), ALU.subtract
                                   ).then_inc(dn_lo_done, 1)

            def pair(i, attend=True, feed=True, more=True, load=False):
                for t in range(ticks):
                    for part in range(3):
                        if attend and part == 1 and t in VALUES and (more or VALUES[t][0] < 2):
                            values_rest(i, *VALUES[t])
                        if attend and part == 2 and t in VALUES and (more or VALUES[t][0] < 2):
                            values_third(i, *VALUES[t])
                        if attend and part == 2 and t in INPUT_NORM and (more or INPUT_NORM[t] == 1):
                            input_rstd(i, INPUT_NORM[t])
                        if attend and (t, part) in Y_STATS:
                            y_rstd_of(i, Y_STATS[t, part])
                        if feed:
                            for kind, a, b in ends.get((t, part), []):
                                if kind == "up":
                                    split_h_lo(i, a)
                                    if i is not pairs or a + 2 < h_tiles:
                                        pool.wait_ge(up_done, h_tiles * (i - 1) + a + 1)
                                        weights_gu_lo(h_tiles * (i - 1) + a + 2, (a + 2) % h_tiles)
                                if kind == "down" and b == T_PAIR - 1 and (i is not pairs or a + 1 < groups):
                                    pool.wait_ge(down_done, T_PAIR * (groups * (i - 1) + a + 1))
                                    weights_dn_lo(groups * (i - 1) + a + 1, (a + 1) % groups)
                        if load and part == 2 and h_tiles <= t < h_tiles + 2:
                            pool.wait_ge(gu_hi_done, t - h_tiles + 1)
                            weights_gu_lo(t - h_tiles, t - h_tiles)
                        if load and part == 2 and t == h_tiles + 2:
                            pool.wait_ge(dn_hi_done, 1)
                            weights_dn_lo(0, 0)

            pool.sem_inc(h_lo_done, 2)
            pool.memset(minus_half[:], -0.5)
            pool.memset(ident[:], 0.0).then_inc(zeroed, 1)
            pool.memset(mask[:], 0.0).then_inc(zeroed, 1)
            pool.memset(v_parts[:].rearrange("p t h a v -> p (t h a v)"), 0.0).then_inc(zeroed, 1)
            pool.wait_ge(zeroed, 3)
            pool.affine_select(out=ident[:], in_=ident[:], compare_op=ALU.not_equal, fill=1.0, base=0,
                               pattern=[[-1, P]], channel_multiplier=1).then_inc(consts_ready, 1)
            pool.affine_select(out=mask[:, P:], in_=mask[:, P:], compare_op=ALU.is_ge, fill=NEG, base=0,
                               pattern=[[-1, P]], channel_multiplier=1).then_inc(consts_ready, 1)
            pool.memset(v_parts[:, :, :, 0, HD], 1.0).then_inc(consts_ready, 1)
            values_rest(0, 0, 0)
            input_rstd(0, 0)
            values_third(0, 0, 0)
            pair(0, feed=False, load=True)
            with pool.Fori(1, pairs - 1) as i:
                pair(i)
            pair(pairs - 1, more=False)
            pair(pairs, attend=False)


def kernel(x, ctx_2048, L0_ffn_w_gate, L0_ffn_w_up, L0_ffn_w_down):
    import numpy as np
    import concourse.bacc as bacc
    from concourse.bass_utils import run_bass_kernel_spmd

    x, ctx = np.ascontiguousarray(x), np.ascontiguousarray(ctx_2048)
    hidden, dim = L0_ffn_w_gate.shape
    h_tiles, kd = hidden // P, dim // P
    gu = np.stack([np.asarray(w).reshape(h_tiles, P, kd, P) for w in (L0_ffn_w_gate, L0_ffn_w_up)])
    gu = np.ascontiguousarray(gu.transpose(1, 4, 0, 3, 2))
    dn = np.ascontiguousarray(np.asarray(L0_ffn_w_down).reshape(dim, h_tiles // 2, 2, P).transpose(1, 3, 2, 0))

    nc = bacc.Bacc("TRN2", target_bir_lowering=False, num_devices=1)
    arrays = {"x_dram": x, "ctx_dram": ctx, "gu_dram": gu, "dn_dram": dn}
    args = [nc.dram_tensor(n, a.shape, mybir.dt.from_np(a.dtype), kind="ExternalInput").ap()
            for n, a in arrays.items()]
    out = nc.dram_tensor("out_dram", x.shape, F32, kind="ExternalOutput").ap()
    build(nc, *args, out)
    r = run_bass_kernel_spmd(nc, [arrays], core_ids=[0])
    return r.results[0]["out_dram"]
```

```python
from contextlib import ExitStack

import concourse.bass as bass
from concourse import mybir

F32 = mybir.dt.float32
F32R = mybir.dt.float32r
BF16 = mybir.dt.bfloat16
F16 = mybir.dt.float16
ALU = mybir.AluOpType
ACT = mybir.ActivationFunctionType
AX = mybir.AxisListType

P = 128
HEADS, HD = 16, 32
EPS = 1e-5
SCALE = HD ** -0.5
NEG = -3.0e38
P_SCALE = 2.0 ** 15
VP = HD + 1

T_PAIR = 4
H_PAIR = 2 * HEADS
FILLS = H_PAIR // 4
LAG_T, LAG_V = 1, 2
MM_TICK = 15
PARTS = (0, 5, 10)
STACK_INC = 16 * 3
USES = FILLS + T_PAIR

INPUT_STATS = {(10, 2): 1, (26, 2): 2}
INPUT_RSTD = {(11, 0): 1, (27, 0): 2}
INPUT_NORM = {(11, 1): 1, (27, 1): 2}
VALUES = {2: (0, 1), 12: (1, 0), 18: (1, 1), 28: (2, 0)}
PIECES_READ = 24
Y_STATS = {(21, 2): 0, (33, 2): 1}
Y_NORM = {(35, 0): 0, (35, 2): 1, (37, 0): 2, (37, 1): 3}
Y_TURNED = {(35, 1): 0, (36, 0): 1, (37, 1): 2, (37, 2): 3}
Y_LO = {(36, 2): 0, (37, 0): 1, (37, 1): 2, (37, 2): 3}


def feed_forward_order(h_tiles, groups, kd):
    per, steps = h_tiles // groups, 3 * kd
    piece = steps // T_PAIR

    def down(g, tile):
        return [("down", g, tile, c) for c in range(3 * per)]

    order = []
    for j in range(h_tiles):
        order += [("gate", j, 0, c) for c in range(steps)]
        for tile in range(T_PAIR):
            if j % per == 0 and j > 0:
                order += down(j // per - 1, tile)
            order += [("up", j, 0, c) for c in range(piece * tile, piece * (tile + 1))]
    for tile in range(T_PAIR):
        order += down(groups - 1, tile)
    return order


def build(nc, x, ctx, gu_w, dn_w, out):
    batches, seq, dim = x.shape
    h_tiles = gu_w.shape[0]
    kd = dim // P
    groups = dn_w.shape[0]
    per = h_tiles // groups
    pairs = batches // 2
    assert seq == 2 * P and dim == HEADS * HD == 4 * P and batches % 2 == 0 and per == 2

    order = feed_forward_order(h_tiles, groups, kd)
    ticks = len(order) // MM_TICK
    assert ticks == 38

    def part_of(n):
        t = min(n // MM_TICK, ticks - 1)
        return t, max(p for p in range(3) if n - MM_TICK * t >= PARTS[p])

    ends = {}
    for n, (kind, a, b, c) in enumerate(order):
        if c == (3 * kd if kind != "down" else 3 * per) - 1:
            ends.setdefault(part_of(n), []).append((kind, a, b))

    x_pair = x.rearrange("(i b) (t p) d -> i p (b t) d", b=2, p=P)
    out_pair = out.rearrange("(i b) (t p) d -> i p (b t) d", b=2, p=P)
    x_batch = x.rearrange("b (t p) d -> b p t d", p=P)
    ctx_batch = ctx.rearrange("b (t p) d -> b p t d", p=P)

    with ExitStack() as stack:
        def sb(name, shape, dt=F32):
            return stack.enter_context(nc.sbuf_tensor(name, shape, dt))

        def ps(name, shape=(P, 512), dt=F32):
            return stack.enter_context(nc.psum_tensor(name, list(shape), dt))

        def sem(name):
            return stack.enter_context(nc.semaphore(name))

        gu_hi = sb("gu_hi", [P, h_tiles, 2, kd, P], F32R)
        dn_hi = sb("dn_hi", [P, h_tiles, dim], F32R)
        gu_raw = sb("gu_raw", [P, 2, kd, P])
        dn_raw = sb("dn_raw", [P, per, dim])
        gu_lo = sb("gu_lo", [P, 2, 2, kd, P], F32R)
        dn_lo = sb("dn_lo", [P, per, dim], F32R)
        yt_hi = sb("yt_hi", [P, kd, T_PAIR * P], F32R)
        yt_lo = sb("yt_lo", [P, kd, T_PAIR * P], F32R)
        h_hi = sb("h_hi", [P, per, T_PAIR * P], F32R)
        h_lo = sb("h_lo", [P, per, T_PAIR * P], F32R)
        h_full = sb("h_full", [P, 2, T_PAIR * P])
        x_ffn = sb("x_ffn", [P, T_PAIR, dim])
        x_att = sb("x_att", [P, T_PAIR, dim])
        x_in = sb("x_in", [P, 2, dim])
        ctx_in = sb("ctx_in", [P, 2, dim])
        split = sb("split", [P, 4, 2 * P], F32R)
        stacks = sb("stacks", [P, 2, 4, 2, 2 * P], F32R)
        v_parts = sb("v_parts", [P, 2, HEADS, 3, VP], BF16)
        v_rest = sb("v_rest", [P, 2, HEADS // 2, HD])
        probs = sb("probs", [P, 2, 3 * P])
        pt_hi = sb("pt_hi", [P, 2, 3 * P], F16)
        pt_lo = sb("pt_lo", [P, 2, 3 * P], F16)
        heads_out = sb("heads_out", [P, 2, 4, VP])
        quotient = sb("quotient", [P, 2, 4])
        y_in = sb("y_in", [P, dim])
        neg_max = sb("neg_max", [P, 2, 2])
        in_stats, y_stats = sb("in_stats", [P, 2, 6]), sb("y_stats", [P, 2, 6])
        in_moments, y_moments = sb("in_moments", [P, 2, 2]), sb("y_moments", [P, T_PAIR, 2])
        in_var, y_var = sb("in_var", [P, 2]), sb("y_var", [P, T_PAIR])
        in_rstd, y_rstd = sb("in_rstd", [P, 2]), sb("y_rstd", [P, T_PAIR])
        minus_half = sb("minus_half", [P, 2])
        mask = sb("mask", [P, 2 * P])
        ident = sb("ident", [P, P])

        gate_ps, up_ps = ps("gate_ps"), ps("up_ps")
        down_ps = [ps("down_ps0"), ps("down_ps1")]
        score_ps, pt_ps, pv_ps, turn_ps = ps("score_ps"), ps("pt_ps"), ps("pv_ps"), ps("turn_ps")

        x_in_loaded, ctx_loaded, x_att_loaded = sem("x_in_loaded"), sem("ctx_loaded"), sem("x_att_loaded")
        x_ffn_loaded, out_stored = sem("x_ffn_loaded"), sem("out_stored")
        gu_loaded, dn_loaded = sem("gu_loaded"), sem("dn_loaded")
        w_loaded = [sem(f"w_loaded{n}") for n in range(4)]
        stack_loaded = [[sem(f"stack_loaded{b}{j}") for j in range(4)] for b in range(2)]
        scores_done, pt_done, pv_done, turned = sem("scores_done"), sem("pt_done"), sem("pv_done"), sem("turned")
        gate_done, up_done, down_done = sem("gate_done"), sem("up_done"), sem("down_done")
        masked, pt_lo_done, pv_reduced = sem("masked"), sem("pt_lo_done"), sem("pv_reduced")
        quotient_done, heads_scaled, x_att_added = sem("quotient_done"), sem("heads_scaled"), sem("x_att_added")
        in_stats_done, in_moments_done, in_var_done, in_normed = (
            sem("in_stats_done"), sem("in_moments_done"), sem("in_var_done"), sem("in_normed"))
        y_stats_done, y_moments_done, y_var_done, y_normed = (
            sem("y_stats_done"), sem("y_moments_done"), sem("y_var_done"), sem("y_normed"))
        turn_lo_done = sem("turn_lo_done")
        gate_free, up_free, down_free = sem("gate_free"), sem("up_free"), sem("down_free")
        exp_done, pt_hi_done, turn_hi_done = sem("exp_done"), sem("pt_hi_done"), sem("turn_hi_done")
        tanh_done, h_hi_done = sem("tanh_done"), sem("h_hi_done")
        v1_done, v2_done = sem("v1_done"), sem("v2_done")
        w_hi_done = [sem("w_hi_even_done"), sem("w_hi_odd_done")]
        zeroed, consts_ready = sem("zeroed"), sem("consts_ready")
        in_rstd_done, y_rstd_done = sem("in_rstd_done"), sem("y_rstd_done")
        v_rest_done, v_ready = sem("v_rest_done"), sem("v_ready")
        h_lo_done, gu_lo_done, dn_lo_done = sem("h_lo_done"), sem("gu_lo_done"), sem("dn_lo_done")

        sp_passed, dve_passed = sem("sp_passed"), sem("dve_passed")

        block = stack.enter_context(nc.Block())


        def starts(i, k=0):
            return isinstance(i, int) and i == 0 and k == 0

        def row(array, i):
            if isinstance(i, int):
                return array[i]
            names = "abcd"[:len(array.shape) - 1]
            return array[bass.ds(i, 1)].rearrange(f"z {' '.join(names)} -> (z a) {' '.join(names[1:])}")

        def fill_at(t, more):
            return t // 4 + 1 if t % 4 == 0 and t < (H_PAIR if more else H_PAIR - 4) else None

        def fill_use(i, g):
            return USES * i + g

        def y_use(i, tile, more):
            return USES * i + (FILLS + 1 if more else FILLS) + tile

        def gates_ended(t, part):
            before = (t, part - 1) if part else (t - 1, 2)
            return [a for kind, a, _ in ends.get(before, []) if kind == "gate"]

        pieces = h_tiles + groups
        half_tiles = T_PAIR // 2
        w_buffers = [gu_raw[:].rearrange("p u k n -> p (u k n)"), dn_raw[:].rearrange("p h d -> p (h d)"),
                     x_ffn[:, 0:half_tiles].rearrange("p t d -> p (t d)"),
                     x_ffn[:, half_tiles:].rearrange("p t d -> p (t d)")]

        def hi_weights(n):
            if n < h_tiles:
                return gu_hi[:, n].rearrange("p u k n -> p (u k n)")
            return dn_hi[:, per * (n - h_tiles):per * (n - h_tiles + 1)].rearrange("p h d -> p (h d)")

        @block.sync
        def _(sp):
            def load_batch(i, b):
                n = 2 * i + b
                if not starts(i, b):
                    sp.wait_ge(turned, USES * i + 4 * b)
                    sp.sem_inc(sp_passed, 1)
                    sp.wait_ge(v_ready, 2 * n)
                    sp.sem_inc(sp_passed, 1)
                sp.dma_start(x_in[:], row(x_batch, n)).then_inc(x_in_loaded, 16)
                sp.dma_start(ctx_in[:], row(ctx_batch, n)).then_inc(ctx_loaded, 16)

            def fill_stack(i, g):
                sp.wait_ge(turn_lo_done, fill_use(i, g) + 1)
                sp.sem_inc(sp_passed, 1)
                if not (isinstance(i, int) and FILLS * i + g < 2):
                    sp.wait_ge(scores_done, H_PAIR * i + 4 * (g - 1))
                for j in range(4):
                    for r, parts in enumerate((slice(0, 3, 2), slice(0, 4, 3), slice(1, 3, 1))):
                        sp.dma_start(stacks[HD * r:HD * r + HD, g % 2, j, :, :].bitcast(F32),
                                     split[HD * j:HD * j + HD, parts, :].bitcast(F32)).then_inc(stack_loaded[g % 2][j], 16)

            def load_gu(j):
                sp.dma_start(gu_raw[:], gu_w[j]).then_inc(gu_loaded, 16)

            def load_dn(k):
                sp.dma_start(dn_raw[:], dn_w[k]).then_inc(dn_loaded, 16)

            def hand_over(i):
                sp.wait_ge(y_normed, T_PAIR * i)
                sp.dma_start(x_ffn[:], x_att[:]).then_inc(x_ffn_loaded, 16)

            def load_pair(i):
                if not starts(i):
                    sp.wait_ge(x_ffn_loaded, 16 * i)
                    sp.sem_inc(sp_passed, 1)
                sp.dma_start(x_att[:], row(x_pair, i)).then_inc(x_att_loaded, 16)

            def attention(i, t, more):
                if t == 8:
                    load_batch(i, 1)
                if t == 24 and more:
                    load_batch(i, 2)
                if fill_at(t, more) is not None:
                    fill_stack(i, fill_at(t, more))

            def feed_forward(i, t, last):
                for part in range(3):
                    for kind, a, b in ends.get((t, part), []):
                        if kind == "up" and not (last and a + 3 >= h_tiles):
                            sp.wait_ge(gu_lo_done, h_tiles * (i - 1) + a + 3)
                            load_gu((a + 3) % h_tiles)
                        if kind == "down" and b == T_PAIR - 1 and not (last and a + 2 >= groups):
                            sp.wait_ge(dn_lo_done, groups * (i - 1) + a + 2)
                            load_dn((a + 2) % groups)

            def store(i):
                for tile in range(T_PAIR):
                    sp.wait_ge(down_free, 2 + groups * T_PAIR * i - T_PAIR + tile + 1)
                    sp.sem_inc(sp_passed, 1)
                    sp.dma_start(row(out_pair, i - 1)[:, tile, :], x_ffn[:, tile, :]).then_inc(out_stored, 16)
                sp.wait_ge(out_stored, 16 * T_PAIR * i)
                sp.sem_inc(sp_passed, 1)

            def load_piece(n):
                if n >= 4:
                    sp.wait_ge(w_hi_done[n % 2], (n - 4) // 2 + 1)
                source = (gu_w[n].rearrange("p u k n -> p (u k n)") if n < h_tiles else
                          dn_w[n - h_tiles].rearrange("p h d -> p (h d)"))
                sp.dma_start(w_buffers[n % 4], source).then_inc(w_loaded[n % 4], 16)

            load_batch(0, 0)
            for n in range(2):
                load_piece(n)
            fill_stack(0, 0)
            for n in range(2, 4):
                load_piece(n)
            load_pair(0)
            for t in range(ticks):
                attention(0, t, True)
                if t + 4 < pieces:
                    load_piece(t + 4)
                if t == PIECES_READ:
                    sp.wait_ge(w_hi_done[0], pieces // 2)
                    load_gu(0)
                    sp.wait_ge(w_hi_done[1], pieces // 2)
                    load_dn(0)
                if t in (PIECES_READ + 1, PIECES_READ + 2):
                    sp.wait_ge(gu_lo_done, t - PIECES_READ)
                    load_gu(t - PIECES_READ)
                if t == PIECES_READ + 3:
                    sp.wait_ge(dn_lo_done, 1)
                    load_dn(1)

            def pair(i, more):
                hand_over(i)
                for t in range(ticks):
                    if t == 2:
                        load_pair(i)
                    attention(i, t, more)
                    feed_forward(i, t - 1, False)
                feed_forward(i, ticks - 1, False)
                store(i)

            with sp.Fori(1, pairs - 1) as i:
                pair(i, True)
            pair(pairs - 1, False)
            hand_over(pairs)
            for t in range(ticks):
                feed_forward(pairs, t, True)
            store(pairs)

        @block.tensor
        def _(pe):
            def turn_qk(i, g):
                if g % 4 == 0:
                    pe.wait_ge(in_normed, 2 * (2 * i + g // 4) + 2)
                    pe.wait_ge(ctx_loaded, 16 * (2 * i + g // 4) + 16)
                if not starts(i, g):
                    pe.wait_ge(turn_lo_done, fill_use(i, g))
                c = (g % 4) * P
                for n, source in enumerate((x_in, ctx_in)):
                    for tile in range(2):
                        mm = pe.transpose(turn_ps[:, (2 * n + tile) * P:(2 * n + tile + 1) * P],
                                          source[:, tile, c:c + P], ident[:])
                mm.then_inc(turned, 1)

            def scores(i, t):
                pe.wait_ge(stack_loaded[t // 4 % 2][t % 4], STACK_INC * (FILLS // 2 * i + t // 8 + 1))
                if not starts(i, t):
                    pe.wait_ge(masked, 2 * (H_PAIR * i + t))
                s = stacks[0:3 * HD, t // 4 % 2, t % 4]
                for tile in range(2):
                    mm = pe.matmul(score_ps[:, tile * 2 * P:(tile + 1) * 2 * P],
                                   s[:, 0, tile * P:(tile + 1) * P], s[:, 1, :], start=True, stop=True)
                mm.then_inc(scores_done, 1)

            def turn_probs(i, t):
                pe.wait_ge(exp_done, 2 * (H_PAIR * i + t) + 2)
                if not starts(i, t):
                    pe.wait_ge(pt_lo_done, H_PAIR * i + t)
                for n in range(3):
                    mm = pe.transpose(pt_ps[:, n * P:(n + 1) * P], probs[:, t % 2, n * P:(n + 1) * P], ident[:])
                mm.then_inc(pt_done, 1)

            def values(i, t):
                if t % 8 == 0:
                    pe.wait_ge(v_ready, 4 * i + t // 8 + 1)
                pe.wait_ge(pt_lo_done, H_PAIR * i + t + 1)
                if not starts(i, t):
                    pe.wait_ge(pv_reduced, H_PAIR * i + t)
                for tile, blocks in enumerate((((0, 0),), ((1, 0), (2, 1)))):
                    for n, (b, keys) in enumerate(blocks):
                        for part in (pt_hi, pt_lo):
                            mm = pe.matmul(pv_ps[:, tile * 3 * VP:(tile + 1) * 3 * VP],
                                           part[:, t % 2, b * P:(b + 1) * P],
                                           v_parts[:, keys, t % HEADS].rearrange("p a v -> p (a v)"),
                                           start=(n == 0 and part is pt_hi),
                                           stop=(n == len(blocks) - 1 and part is pt_lo))
                mm.then_inc(pv_done, 1)

            def turn_y(i, tile, more):
                pe.wait_ge(y_normed, T_PAIR * i + tile + 1)
                if tile != 1:
                    pe.wait_ge(turn_lo_done, y_use(i, tile, more) - (1 if tile else 0))
                for k in range(kd):
                    mm = pe.transpose((turn_ps, score_ps)[tile % 2][:, k * P:(k + 1) * P],
                                      y_in[:, k * P:(k + 1) * P], ident[:])
                mm.then_inc(turned, 1)

            def product(i, n):
                kind, a, b, c = order[n]
                if kind == "down":
                    hh, term = divmod(c, 3)
                    term = (0, 2, 1)[term]
                    if c == 0:
                        pe.wait_ge(down_free, groups * T_PAIR * (i - 1) + a * T_PAIR + b + 1)
                    if b == 0 and c == 0:
                        pe.wait_ge(dn_lo_done, groups * (i - 1) + a + 1)
                    if b == 0 and term == 0:
                        pe.wait_ge(h_hi_done, h_tiles * (i - 1) + per * a + hh + 1)
                    if b == 0 and term == 1:
                        pe.wait_ge(h_lo_done, 2 + h_tiles * (i - 1) + per * a + hh + 1)
                    mm = pe.matmul(down_ps[b % 2][:], (h_lo if term == 1 else h_hi)[:, hh, b * P:(b + 1) * P],
                                   dn_lo[:, hh] if term == 2 else dn_hi[:, per * a + hh],
                                   start=(c == 0), stop=(c == 3 * per - 1))
                    if c == 3 * per - 1:
                        mm.then_inc(down_done, 1)
                    return
                u = 0 if kind == "gate" else 1
                k, term = divmod(c, 3)
                if c == 0:
                    pe.wait_ge((gate_free, up_free)[u], h_tiles * (i - 1) + a + 1)
                if c == 0 and u == 0:
                    pe.wait_ge(gu_lo_done, h_tiles * (i - 1) + a + 1)
                mm = pe.matmul((gate_ps, up_ps)[u][:],
                               gu_lo[:, a % 2, u, k] if term == 2 else gu_hi[:, a, u, k],
                               (yt_lo if term == 1 else yt_hi)[:, k, :], start=(c == 0), stop=(c == 3 * kd - 1))
                if c == 3 * kd - 1:
                    mm.then_inc((gate_done, up_done)[u], 1)

            def pair(i, attend=True, feed=True, more=True):
                if feed:
                    pe.wait_ge(turn_lo_done, USES * i + (1 if attend else 0))
                for t in range(ticks):
                    for part in range(3):
                        if attend and part == 0 and t < H_PAIR:
                            scores(i, t)
                        if attend and part == 0 and fill_at(t, more) is not None:
                            turn_qk(i, fill_at(t, more))
                        if attend and part == 1 and 0 <= t - LAG_T < H_PAIR:
                            turn_probs(i, t - LAG_T)
                        if attend and part == 2 and 0 <= t - LAG_V < H_PAIR:
                            values(i, t - LAG_V)
                        if attend and (t, part) in Y_TURNED:
                            turn_y(i, Y_TURNED[t, part], more)
                        if feed:
                            for n in range(len(order)):
                                if part_of(n) == (t, part):
                                    product(i, n)

            pe.wait_ge(consts_ready, 3)
            turn_qk(0, 0)
            pair(0, feed=False)
            pe.wait_ge(w_hi_done[0], pieces // 2)
            pe.wait_ge(w_hi_done[1], pieces // 2)
            with pe.Fori(1, pairs - 1) as i:
                pair(i)
            pair(pairs - 1, more=False)
            pair(pairs, attend=False)

        @block.vector
        def _(dve):
            def input_stats(i, b):
                n = 2 * i + b
                dve.wait_ge(x_in_loaded, 16 * n + 16)
                for tile in range(2):
                    dve.bn_stats(in_stats[:, tile, :], x_in[:, tile, :]).then_inc(in_stats_done, 1)
                dve.wait_ge(in_stats_done, 2 * n + 2)
                dve.sem_inc(dve_passed, 1)
                for tile in range(2):
                    dve.bn_aggr(in_moments[:, tile, :], in_stats[:, tile, :]).then_inc(in_moments_done, 1)
                dve.wait_ge(in_moments_done, 2 * n + 2)
                dve.tensor_scalar(in_var[:], in_moments[:, :, 1], EPS, None, ALU.add).then_inc(in_var_done, 1)

            def input_norm(i, b):
                dve.wait_ge(in_rstd_done, 2 * i + b + 1)
                for tile in range(2):
                    dve.tensor_scalar(x_in[:, tile, :], x_in[:, tile, :], in_moments[:, tile, 0:1],
                                      in_rstd[:, tile:tile + 1], ALU.subtract, ALU.mult).then_inc(in_normed, 1)

            def y_stats_of(i, half):
                dve.wait_ge(x_att_added, FILLS * i + 4 * half + 4)
                for tile in range(2):
                    dve.bn_stats(y_stats[:, tile, :], x_att[:, 2 * half + tile, :]).then_inc(y_stats_done, 1)
                dve.wait_ge(y_stats_done, 4 * i + 2 * half + 2)
                dve.sem_inc(dve_passed, 1)
                for tile in range(2):
                    dve.bn_aggr(y_moments[:, 2 * half + tile, :], y_stats[:, tile, :]).then_inc(y_moments_done, 1)
                dve.wait_ge(y_moments_done, 4 * i + 2 * half + 2)
                dve.tensor_scalar(y_var[:, 2 * half:2 * half + 2], y_moments[:, 2 * half:2 * half + 2, 1], EPS, None, ALU.add).then_inc(y_var_done, 1)

            def y_norm(i, tile, more):
                if tile % 2 == 0:
                    dve.wait_ge(y_rstd_done, 2 * i + tile // 2 + 1)
                if tile:
                    dve.wait_ge(turned, y_use(i, tile, more))
                dve.tensor_scalar(y_in[:], x_att[:, tile, :], y_moments[:, tile, 0:1],
                                  y_rstd[:, tile:tile + 1], ALU.subtract, ALU.mult).then_inc(y_normed, 1)

            def mask_scores(i, t):
                dve.wait_ge(scores_done, H_PAIR * i + t + 1)
                if not (isinstance(i, int) and H_PAIR * i + t < 2):
                    dve.wait_ge(pt_done, H_PAIR * i + t - 1)
                dve.sem_inc(dve_passed, 1)
                for tile, (lo, hi, m) in enumerate(((0, P, P), (P, 3 * P, 0))):
                    dve.tensor_tensor_reduce(probs[:, t % 2, lo:hi], score_ps[:, tile * 2 * P:tile * 2 * P + hi - lo],
                                             mask[:, m:], -SCALE, -NEG, ALU.add, ALU.min,
                                             neg_max[:, t % 2, tile:tile + 1]).then_inc(masked, 1)

            def split_qk_lo(i, g):
                use = fill_use(i, g)
                dve.wait_ge(turn_hi_done, use + 1)
                dve.tensor_tensor(split[:, 1:4:2, :], turn_ps[:].rearrange("p (a n) -> p a n", a=2),
                                  split[:, 0:4:2, :].bitcast(F32), ALU.subtract).then_inc(turn_lo_done, 1)

            def split_y_lo(i, tile, more):
                dve.wait_ge(turn_hi_done, y_use(i, tile, more) + 1)
                cols = slice(tile * P, (tile + 1) * P)
                dve.tensor_tensor(yt_lo[:, :, cols], (turn_ps, score_ps)[tile % 2][:].rearrange("p (k n) -> p k n", k=kd),
                                  yt_hi[:, :, cols].bitcast(F32), ALU.subtract).then_inc(turn_lo_done, 1)

            def split_probs_lo(i, t):
                dve.wait_ge(pt_hi_done, H_PAIR * i + t + 1)
                dve.scalar_tensor_tensor(out=pt_lo[:, t % 2, :], in0=pt_ps[:, 0:3 * P], scalar=P_SCALE,
                                         in1=pt_hi[:, t % 2, :], op0=ALU.mult, op1=ALU.subtract
                                         ).then_inc(pt_lo_done, 1)

            def collect_head(i, t):
                dve.wait_ge(pv_done, H_PAIR * i + t + 1)
                if t % 4 == 0 and not starts(i, t):
                    dve.wait_ge(x_att_added, FILLS * i + t // 4)
                dve.tensor_reduce(heads_out[:, :, t % 4, :],
                                  pv_ps[:, 0:6 * VP].rearrange("p (q a v) -> p q v a", q=2, a=3),
                                  AX.X, ALU.add).then_inc(pv_reduced, 1)
                if t % 4 < 3:
                    return
                g = t // 4
                dve.wait_ge(pv_reduced, H_PAIR * i + t + 1)
                dve.reciprocal(quotient[:], heads_out[:, :, :, HD]).then_inc(quotient_done, 1)
                dve.wait_ge(quotient_done, FILLS * i + g + 1)
                dve.tensor_tensor(heads_out[:, :, :, 0:HD], heads_out[:, :, :, 0:HD],
                                  quotient[:].unsqueeze(3).broadcast_to([P, 2, 4, HD]), ALU.mult
                                  ).then_inc(heads_scaled, 1)
                if g == 0:
                    dve.wait_ge(x_att_loaded, 16 * i + 16)
                dve.wait_ge(heads_scaled, FILLS * i + g + 1)
                xs = x_att[:, 2 * (g // 4):2 * (g // 4) + 2, (g % 4) * P:(g % 4 + 1) * P].rearrange(
                    "p q (h d) -> p q h d", h=4)
                dve.tensor_tensor(xs, xs, heads_out[:, :, :, 0:HD], ALU.add).then_inc(x_att_added, 1)

            def gated(i, j):
                n = h_tiles * (i - 1) + j
                dve.wait_ge(tanh_done, n + 1)
                hf = h_full[:, j % 2, :]
                dve.scalar_tensor_tensor(out=hf, in0=hf, scalar=1.0, in1=gate_ps[:], op0=ALU.add, op1=ALU.mult
                                         ).then_inc(gate_free, 1)

            def hidden(i, j):
                n = h_tiles * (i - 1) + j
                dve.wait_ge(up_done, n + 1)
                dve.wait_ge(gate_free, n + 2)
                hf = h_full[:, j % 2, :]
                dve.scalar_tensor_tensor(out=hf, in0=hf, scalar=0.5, in1=up_ps[:], op0=ALU.mult, op1=ALU.mult
                                         ).then_inc(up_free, 1)

            def add_down(i, k, tile):
                n = groups * T_PAIR * (i - 1) + T_PAIR * k + tile
                dve.wait_ge(down_done, n + 1)
                if k == 0 and tile == 0:
                    dve.wait_ge(x_ffn_loaded, 16 * i)
                if k:
                    dve.wait_ge(down_free, 2 + n - T_PAIR + 1)
                dve.tensor_tensor(x_ffn[:, tile, :], x_ffn[:, tile, :], down_ps[tile % 2][:], ALU.add
                                  ).then_inc(down_free, 1)

            def weights_hi(n):
                dve.wait_ge(w_loaded[n % 4], 16 * (n // 4) + 16)
                dve.tensor_copy(hi_weights(n), w_buffers[n % 4]).then_inc(w_hi_done[1], 1)

            def pair(i, attend=True, feed=True, more=True, load=False):
                for t in range(ticks):
                    for part in range(3):
                        if load and part == 2 and t < pieces and t % 2 == 1:
                            weights_hi(t)
                        if attend and part == 0 and t < H_PAIR:
                            mask_scores(i, t)
                        if attend and part == 1 and fill_at(t, more) is not None:
                            split_qk_lo(i, fill_at(t, more))
                        if attend and part == (2 if feed else 1) and 0 <= t - LAG_T < H_PAIR:
                            split_probs_lo(i, t - LAG_T)
                        if attend and part == 2 and 0 <= t - LAG_V < H_PAIR:
                            collect_head(i, t - LAG_V)
                        if attend and (t, part) in INPUT_STATS and (more or INPUT_STATS[t, part] == 1):
                            input_stats(i, INPUT_STATS[t, part])
                        if attend and (t, part) in INPUT_NORM and (more or INPUT_NORM[t, part] == 1):
                            input_norm(i, INPUT_NORM[t, part])
                        if attend and (t, part) in Y_STATS:
                            y_stats_of(i, Y_STATS[t, part])
                        if attend and (t, part) in Y_NORM:
                            y_norm(i, Y_NORM[t, part], more)
                        if feed:
                            for j in gates_ended(t, part):
                                gated(i, j)
                            for kind, a, b in ends.get((t, part), []):
                                if kind == "up":
                                    hidden(i, a)
                                if kind == "down":
                                    add_down(i, a, b)
                        if attend and (t, part) in Y_LO:
                            split_y_lo(i, Y_LO[t, part], more)

            dve.sem_inc(gate_free, 1)
            dve.sem_inc(up_free, 1)
            dve.sem_inc(down_free, 2)
            dve.wait_ge(consts_ready, 3)
            input_stats(0, 0)
            input_norm(0, 0)
            split_qk_lo(0, 0)
            pair(0, feed=False, load=True)
            with dve.Fori(1, pairs - 1) as i:
                pair(i)
            pair(pairs - 1, more=False)
            pair(pairs, attend=False)

        @block.scalar
        def _(act):
            def exponentials(i, t):
                for tile, (lo, hi) in enumerate(((0, P), (P, 3 * P))):
                    act.wait_ge(masked, 2 * (H_PAIR * i + t) + tile + 1)
                    p = probs[:, t % 2, lo:hi]
                    act.activation(p, p, ACT.Exp, bias=neg_max[:, t % 2, tile:tile + 1], scale=-1.0
                                   ).then_inc(exp_done, 1)

            def split_qk_hi(i, g):
                act.wait_ge(turned, fill_use(i, g) + 1)
                if not starts(i, g):
                    for j in range(4):
                        act.wait_ge(stack_loaded[(g - 1) % 2][j], STACK_INC * (FILLS // 2 * i + (g - 1) // 2 + 1))
                act.activation(split[:, 0:4:2, :], turn_ps[:].rearrange("p (a n) -> p a n", a=2), ACT.Copy
                               ).then_inc(turn_hi_done, 1)

            def split_y_hi(i, tile, more):
                act.wait_ge(turned, y_use(i, tile, more) + 1)
                if tile == 0 and not starts(i):
                    act.wait_ge(up_done, h_tiles * i)
                act.activation(yt_hi[:, :, tile * P:(tile + 1) * P],
                               (turn_ps, score_ps)[tile % 2][:].rearrange("p (k n) -> p k n", k=kd), ACT.Copy
                               ).then_inc(turn_hi_done, 1)

            def split_probs_hi(i, t):
                act.wait_ge(pt_done, H_PAIR * i + t + 1)
                if not (isinstance(i, int) and H_PAIR * i + t < 2):
                    act.wait_ge(pv_done, H_PAIR * i + t - 1)
                act.activation(pt_hi[:, t % 2, :], pt_ps[:, 0:3 * P], ACT.Copy, scale=P_SCALE
                               ).then_inc(pt_hi_done, 1)

            def values_first(i, b, half):
                n = 2 * i + b
                act.wait_ge(ctx_loaded, 16 * n + 16)
                if not starts(i, b):
                    act.wait_ge(pv_done, HEADS * n - HEADS // 2 + 8 * half)
                h = slice(8 * half, 8 * half + 8)
                act.activation(v_parts[:, :, h, 0, 0:HD],
                               ctx_in[:].rearrange("p t (h d) -> p t h d", h=HEADS)[:, :, h, :], ACT.Copy
                               ).then_inc(v1_done, 1)

            def values_second(i, b, half):
                act.wait_ge(v_rest_done, 2 * (2 * i + b) + half + 1)
                act.activation(v_parts[:, :, 8 * half:8 * half + 8, 1, 0:HD], v_rest[:], ACT.Copy
                               ).then_inc(v2_done, 1)

            def tanh(i, j):
                n = h_tiles * (i - 1) + j
                act.wait_ge(gate_done, n + 1)
                act.wait_ge(h_lo_done, n + 1)
                act.activation(h_full[:, j % 2, :], gate_ps[:], ACT.Tanh, scale=0.5).then_inc(tanh_done, 1)

            def split_h_hi(i, j):
                act.wait_ge(up_free, h_tiles * (i - 1) + j + 2)
                act.activation(h_hi[:, j % per, :], h_full[:, j % 2, :], ACT.Copy).then_inc(h_hi_done, 1)

            def weights_hi(n):
                act.wait_ge(w_loaded[n % 4], 16 * (n // 4) + 16)
                act.activation(hi_weights(n), w_buffers[n % 4], ACT.Copy).then_inc(w_hi_done[0], 1)

            def pair(i, attend=True, feed=True, more=True, load=False):
                for t in range(ticks):
                    for part in range(3):
                        if attend and part == 0 and fill_at(t, more) is not None:
                            split_qk_hi(i, fill_at(t, more))
                        if attend and part == 1 and 0 <= t - LAG_T < H_PAIR:
                            split_probs_hi(i, t - LAG_T)
                        if attend and part == 1 and t < H_PAIR:
                            exponentials(i, t)
                        if attend and part == 1 and t in VALUES and (more or VALUES[t][0] < 2):
                            values_first(i, *VALUES[t])
                        if attend and part == 2 and t in VALUES and (more or VALUES[t][0] < 2):
                            values_second(i, *VALUES[t])
                        if feed:
                            for kind, a, b in ends.get((t, part), []):
                                if kind == "gate":
                                    tanh(i, a)
                                if kind == "up":
                                    split_h_hi(i, a)
                        if attend and (t, part) in Y_LO:
                            split_y_hi(i, Y_LO[t, part], more)
                        if load and part == 2 and t < pieces and t % 2 == 0:
                            weights_hi(t)

            act.wait_ge(consts_ready, 3)
            values_first(0, 0, 0)
            split_qk_hi(0, 0)
            values_second(0, 0, 0)
            pair(0, feed=False, load=True)
            with act.Fori(1, pairs - 1) as i:
                pair(i)
            pair(pairs - 1, more=False)
            pair(pairs, attend=False)

        @block.gpsimd
        def _(pool):
            def input_rstd(i, b):
                pool.wait_ge(in_var_done, 2 * i + b + 1)
                pool.tensor_tensor(in_rstd[:], in_var[:], minus_half[:], ALU.pow).then_inc(in_rstd_done, 1)

            def y_rstd_of(i, half):
                pool.wait_ge(y_var_done, 2 * i + half + 1)
                pool.tensor_tensor(y_rstd[:, 2 * half:2 * half + 2], y_var[:, 2 * half:2 * half + 2], minus_half[:], ALU.pow).then_inc(y_rstd_done, 1)

            def values_rest(i, b, half):
                h = slice(8 * half, 8 * half + 8)
                pool.wait_ge(v1_done, 2 * (2 * i + b) + half + 1)
                if not starts(i, 2 * b + half):
                    pool.wait_ge(v_ready, 2 * (2 * i + b) + half)
                pool.tensor_tensor(v_rest[:], ctx_in[:].rearrange("p t (h d) -> p t h d", h=HEADS)[:, :, h, :],
                                   v_parts[:, :, h, 0, 0:HD], ALU.subtract).then_inc(v_rest_done, 1)

            def values_third(i, b, half):
                pool.wait_ge(v2_done, 2 * (2 * i + b) + half + 1)
                h = slice(8 * half, 8 * half + 8)
                pool.tensor_tensor(v_parts[:, :, h, 2, 0:HD], v_rest[:], v_parts[:, :, h, 1, 0:HD],
                                   ALU.subtract).then_inc(v_ready, 1)

            def split_h_lo(i, j):
                pool.wait_ge(h_hi_done, h_tiles * (i - 1) + j + 1)
                pool.tensor_tensor(h_lo[:, j % per, :], h_full[:, j % 2, :], h_hi[:, j % per, :].bitcast(F32),
                                   ALU.subtract).then_inc(h_lo_done, 1)

            def weights_gu_lo(n, j):
                pool.wait_ge(gu_loaded, 16 * (n + 1))
                pool.tensor_tensor(gu_lo[:, j % 2].rearrange("p u k n -> p (u k n)"),
                                   gu_raw[:].rearrange("p u k n -> p (u k n)"),
                                   gu_hi[:, j].bitcast(F32).rearrange("p u k n -> p (u k n)"), ALU.subtract
                                   ).then_inc(gu_lo_done, 1)

            def weights_dn_lo(n, k):
                pool.wait_ge(dn_loaded, 16 * (n + 1))
                pool.tensor_tensor(dn_lo[:], dn_raw[:], dn_hi[:, per * k:per * (k + 1)].bitcast(F32), ALU.subtract
                                   ).then_inc(dn_lo_done, 1)

            def pair(i, attend=True, feed=True, more=True, load=False):
                for t in range(ticks):
                    for part in range(3):
                        if attend and part == 1 and t in VALUES and (more or VALUES[t][0] < 2):
                            values_rest(i, *VALUES[t])
                        if attend and part == 2 and t in VALUES and (more or VALUES[t][0] < 2):
                            values_third(i, *VALUES[t])
                        if attend and (t, part) in INPUT_RSTD and (more or INPUT_RSTD[t, part] == 1):
                            input_rstd(i, INPUT_RSTD[t, part])
                        if attend and (t, part) in Y_STATS:
                            y_rstd_of(i, Y_STATS[t, part])
                        if feed:
                            for kind, a, b in ends.get((t, part), []):
                                if kind == "up":
                                    split_h_lo(i, a)
                                    if i is not pairs or a + 2 < h_tiles:
                                        pool.wait_ge(up_done, h_tiles * (i - 1) + a + 1)
                                        weights_gu_lo(h_tiles * (i - 1) + a + 2, (a + 2) % h_tiles)
                                if kind == "down" and b == T_PAIR - 1 and (i is not pairs or a + 1 < groups):
                                    pool.wait_ge(down_done, T_PAIR * (groups * (i - 1) + a + 1))
                                    weights_dn_lo(groups * (i - 1) + a + 1, (a + 1) % groups)
                        if load and (t, part) == (PIECES_READ, 2):
                            pool.wait_ge(w_hi_done[0], pieces // 2)
                            pool.wait_ge(w_hi_done[1], pieces // 2)
                            weights_gu_lo(0, 0)
                        if load and (t, part) == (PIECES_READ + 1, 2):
                            weights_gu_lo(1, 1)
                        if load and (t, part) == (PIECES_READ + 2, 2):
                            weights_dn_lo(0, 0)

            pool.sem_inc(h_lo_done, 2)
            pool.memset(minus_half[:], -0.5)
            pool.memset(ident[:], 0.0).then_inc(zeroed, 1)
            pool.memset(mask[:], 0.0).then_inc(zeroed, 1)
            pool.memset(v_parts[:].rearrange("p t h a v -> p (t h a v)"), 0.0).then_inc(zeroed, 1)
            pool.wait_ge(zeroed, 3)
            pool.affine_select(out=ident[:], in_=ident[:], compare_op=ALU.not_equal, fill=1.0, base=0,
                               pattern=[[-1, P]], channel_multiplier=1).then_inc(consts_ready, 1)
            pool.affine_select(out=mask[:, P:], in_=mask[:, P:], compare_op=ALU.is_ge, fill=NEG, base=0,
                               pattern=[[-1, P]], channel_multiplier=1).then_inc(consts_ready, 1)
            pool.memset(v_parts[:, :, :, 0, HD], 1.0).then_inc(consts_ready, 1)
            values_rest(0, 0, 0)
            input_rstd(0, 0)
            values_third(0, 0, 0)
            pair(0, feed=False, load=True)
            with pool.Fori(1, pairs - 1) as i:
                pair(i)
            pair(pairs - 1, more=False)
            pair(pairs, attend=False)


def kernel(x, ctx_2048, L0_ffn_w_gate, L0_ffn_w_up, L0_ffn_w_down):
    import numpy as np
    import concourse.bacc as bacc
    from concourse.bass_utils import run_bass_kernel_spmd

    x, ctx = np.ascontiguousarray(x), np.ascontiguousarray(ctx_2048)
    hidden, dim = L0_ffn_w_gate.shape
    h_tiles, kd = hidden // P, dim // P
    gu = np.stack([np.asarray(w).reshape(h_tiles, P, kd, P) for w in (L0_ffn_w_gate, L0_ffn_w_up)])
    gu = np.ascontiguousarray(gu.transpose(1, 4, 0, 3, 2))
    dn = np.ascontiguousarray(np.asarray(L0_ffn_w_down).reshape(dim, h_tiles // 2, 2, P).transpose(1, 3, 2, 0))

    nc = bacc.Bacc("TRN2", target_bir_lowering=False, num_devices=1)
    arrays = {"x_dram": x, "ctx_dram": ctx, "gu_dram": gu, "dn_dram": dn}
    args = [nc.dram_tensor(n, a.shape, mybir.dt.from_np(a.dtype), kind="ExternalInput").ap()
            for n, a in arrays.items()]
    out = nc.dram_tensor("out_dram", x.shape, F32, kind="ExternalOutput").ap()
    build(nc, *args, out)
    r = run_bass_kernel_spmd(nc, [arrays], core_ids=[0])
    return r.results[0]["out_dram"]
```

```python
from collections import namedtuple
from contextlib import ExitStack

import concourse.bass as bass
from concourse import mybir

F32 = mybir.dt.float32
F32R = mybir.dt.float32r
BF16 = mybir.dt.bfloat16
F16 = mybir.dt.float16
ALU = mybir.AluOpType
ACT = mybir.ActivationFunctionType
AX = mybir.AxisListType

P = 128
HEADS, HD = 16, 32
EPS = 1e-5
SCALE = HD ** -0.5
NEG = -3.0e38
P_SCALE = 2.0 ** 15
VP = HD + 1

T_PAIR = 4
H_PAIR = 2 * HEADS
FILLS = H_PAIR // 4
LAG_T, LAG_V = 1, 2
TICKS = H_PAIR + 6
MM_TICK = {4: 15, 2: 13}
STACK_INC = 16 * 3
USES = FILLS + T_PAIR

Step = namedtuple("Step", "heads batches y_tiles fed")
FIRST = Step(range(HEADS, H_PAIR), 2, (2, 3), ())
SECOND = Step(range(H_PAIR), 2, (0, 1, 2, 3), (2, 3))
MIDDLE = Step(range(H_PAIR), 2, (0, 1, 2, 3), (0, 1, 2, 3))
LAST_HEADS = Step(range(HEADS), 0, (0, 1), (0, 1, 2, 3))
LAST = Step(range(0), -1, (), (0, 1))

INPUT_STATS = {(9, 2): (1, 0), (10, 1): (1, 1), (25, 2): (2, 0), (26, 1): (2, 1)}
INPUT_MOMENTS = {(10, 2): 1, (26, 2): 2}
INPUT_RSTD = INPUT_MOMENTS
INPUT_NORM = {(11, 1): 1, (27, 1): 2}
VALUES_1 = {(2, 1): (0, 1), (12, 1): (1, 0), (18, 1): (1, 1), (28, 1): (2, 0)}
VALUES_2 = {(t + 1, 2): which for (t, _), which in VALUES_1.items()}
VALUES_3 = {(t + 2, 0): which for (t, _), which in VALUES_1.items()}
Y_STATS = {(18, 2): 0, (19, 2): 1, (33, 2): 2, (34, 0): 3}
Y_MOMENTS = {(20, 0): 0, (34, 0): 1}
Y_RSTD = Y_MOMENTS
Y_NORM = {(30, 1): 0, (32, 1): 1, (34, 2): 2, (35, 1): 3}
Y_TURNED = {(31, 0): 0, (33, 0): 1, (35, 1): 2, (36, 0): 3}
Y_SPLIT = {(36, 2): 0, (37, 0): 1, (37, 1): 2, (37, 2): 3}
Y_SPLIT_SECOND = {(34, 1): 0, (35, 0): 1, (36, 0): 2, (36, 1): 3}
W_BUFFERS = 6
PIECES_READ = 33
LO_MADE = (34, 2)


def feed_forward_order(h_tiles, groups, kd, tiles):
    per, steps = h_tiles // groups, 3 * kd
    piece = steps // len(tiles)

    def down(g, tile):
        return [("down", g, tile, c) for c in range(3 * per)]

    order = []
    for j in range(h_tiles):
        order += [("gate", j, 0, c) for c in range(steps)]
        for n, tile in enumerate(tiles):
            if j % per == 0 and j > 0:
                order += down(j // per - 1, tile)
            order += [("up", j, 0, c) for c in range(piece * n, piece * (n + 1))]
    assert per == 2 and len(tiles) in (2, 4)
    together = [(n, c) for n in range(3) for c in range(3)]
    together += [(0, 3), (0, 4), (1, 3), (1, 4), (2, 3), (0, 5), (2, 4), (1, 5), (2, 5)]
    order += [("down", groups - 1, tiles[n], c) for n, c in together if n < len(tiles)]
    for tile in tiles[3:]:
        order += down(groups - 1, tile)
    return order


def build(nc, x, ctx, gu_w, dn_w, out):
    batches, seq, dim = x.shape
    h_tiles = gu_w.shape[0]
    kd = dim // P
    groups = dn_w.shape[0]
    per = h_tiles // groups
    pairs = batches // 2
    assert seq == 2 * P and dim == HEADS * HD == 4 * P and batches % 2 == 0 and per == 2

    orders = {tiles: feed_forward_order(h_tiles, groups, kd, tiles) for tiles in (SECOND.fed, MIDDLE.fed, LAST.fed)}

    def part_of(tiles, n):
        m = MM_TICK[len(tiles)]
        t = min(n // m, TICKS - 1)
        return t, min((n - m * t) // (m // 3), 2)

    ends = {(): {}}
    for tiles, order in orders.items():
        ends[tiles] = {}
        for n, (kind, a, b, c) in enumerate(order):
            if c == (3 * kd if kind != "down" else 3 * per) - 1:
                ends[tiles].setdefault(part_of(tiles, n), []).append((kind, a, b))

    x_pair = x[1:batches - 1].rearrange("(i b) (t p) d -> i p (b t) d", b=2, p=P)
    out_pair = out[1:batches - 1].rearrange("(i b) (t p) d -> i p (b t) d", b=2, p=P)
    out_batch = out.rearrange("b (t p) d -> b p t d", p=P)
    x_batch = x.rearrange("b (t p) d -> b p t d", p=P)
    ctx_batch = ctx.rearrange("b (t p) d -> b p t d", p=P)

    with ExitStack() as stack:
        def sb(name, shape, dt=F32):
            return stack.enter_context(nc.sbuf_tensor(name, shape, dt))

        def ps(name, shape=(P, 512), dt=F32):
            return stack.enter_context(nc.psum_tensor(name, list(shape), dt))

        def sem(name):
            return stack.enter_context(nc.semaphore(name))

        gu_hi = sb("gu_hi", [P, h_tiles, 2, kd, P], F32R)
        dn_hi = sb("dn_hi", [P, h_tiles, dim], F32R)
        gu_raw = sb("gu_raw", [P, 2, kd, P])
        dn_raw = sb("dn_raw", [P, per, dim])
        gu_lo = sb("gu_lo", [P, 2, 2, kd, P], F32R)
        dn_lo = sb("dn_lo", [P, per, dim], F32R)
        yt_hi = sb("yt_hi", [P, kd, T_PAIR * P], F32R)
        yt_lo = sb("yt_lo", [P, kd, T_PAIR * P], F32R)
        h_hi = sb("h_hi", [P, per, T_PAIR * P], F32R)
        h_lo = sb("h_lo", [P, per, T_PAIR * P], F32R)
        h_full = sb("h_full", [P, 2, T_PAIR * P])
        x_ffn = sb("x_ffn", [P, T_PAIR, dim])
        x_att = sb("x_att", [P, T_PAIR, dim])
        x_in = sb("x_in", [P, 2, dim])
        ctx_in = sb("ctx_in", [P, 2, dim])
        split = sb("split", [P, 4, 2 * P], F32R)
        stacks = sb("stacks", [P, 2, 4, 2, 2 * P], F32R)
        v_parts = sb("v_parts", [P, 2, HEADS, 3, VP], BF16)
        v_rest = sb("v_rest", [P, 2, HEADS // 2, HD])
        probs = sb("probs", [P, 2, 3 * P])
        pt_hi = sb("pt_hi", [P, 2, 3 * P], F16)
        pt_lo = sb("pt_lo", [P, 2, 3 * P], F16)
        heads_out = sb("heads_out", [P, 2, 4, VP])
        quotient = sb("quotient", [P, 2, 4])
        y_in = sb("y_in", [P, dim])
        neg_max = sb("neg_max", [P, 2, 2])
        in_stats, y_stats = sb("in_stats", [P, 2, 6]), sb("y_stats", [P, 2, 6])
        in_moments, y_moments = sb("in_moments", [P, 2, 2]), sb("y_moments", [P, T_PAIR, 2])
        in_var, y_var = sb("in_var", [P, 2]), sb("y_var", [P, T_PAIR])
        in_rstd, y_rstd = sb("in_rstd", [P, 2]), sb("y_rstd", [P, T_PAIR])
        minus_half = sb("minus_half", [P, 2])
        mask = sb("mask", [P, 2 * P])
        ident = sb("ident", [P, P])

        gate_ps, up_ps = ps("gate_ps"), ps("up_ps")
        down_ps = [ps("down_ps0"), ps("down_ps1")]
        score_ps, pt_ps, pv_ps, turn_ps = ps("score_ps"), ps("pt_ps"), ps("pv_ps"), ps("turn_ps")
        y_ps = (turn_ps, score_ps, pt_ps, pv_ps)

        x_in_loaded, ctx_loaded, x_att_loaded = sem("x_in_loaded"), sem("ctx_loaded"), sem("x_att_loaded")
        x_ffn_loaded, out_stored = sem("x_ffn_loaded"), sem("out_stored")
        gu_loaded, gu_spare_loaded, dn_loaded = sem("gu_loaded"), sem("gu_spare_loaded"), sem("dn_loaded")
        w_loaded = [sem(f"w_loaded{n}") for n in range(W_BUFFERS)]
        stack_loaded = [[sem(f"stack_loaded{b}{j}") for j in range(4)] for b in range(2)]
        scores_done, pt_done, pv_done, turned = sem("scores_done"), sem("pt_done"), sem("pv_done"), sem("turned")
        gate_done, up_done, down_done = sem("gate_done"), sem("up_done"), sem("down_done")
        masked, pt_lo_done, pv_reduced = sem("masked"), sem("pt_lo_done"), sem("pv_reduced")
        quotient_done, heads_scaled, x_att_added = sem("quotient_done"), sem("heads_scaled"), sem("x_att_added")
        in_stats_done, in_moments_done, in_var_done, in_normed = (
            sem("in_stats_done"), sem("in_moments_done"), sem("in_var_done"), sem("in_normed"))
        y_stats_done, y_moments_done, y_var_done, y_normed = (
            sem("y_stats_done"), sem("y_moments_done"), sem("y_var_done"), sem("y_normed"))
        turn_lo_done = sem("turn_lo_done")
        gate_free, up_free, down_free = sem("gate_free"), sem("up_free"), sem("down_free")
        exp_done, pt_hi_done, turn_hi_done = sem("exp_done"), sem("pt_hi_done"), sem("turn_hi_done")
        tanh_done, h_hi_done = sem("tanh_done"), sem("h_hi_done")
        v1_done, v2_done = sem("v1_done"), sem("v2_done")
        w_hi_done = [sem("w_hi_even_done"), sem("w_hi_odd_done")]
        zeroed, consts_ready = sem("zeroed"), sem("consts_ready")
        in_rstd_done, y_rstd_done = sem("in_rstd_done"), sem("y_rstd_done")
        v_rest_done, v_ready = sem("v_rest_done"), sem("v_ready")
        h_lo_done, gu_lo_done, dn_lo_done = sem("h_lo_done"), sem("gu_lo_done"), sem("dn_lo_done")

        sp_passed, dve_passed = sem("sp_passed"), sem("dve_passed")

        block = stack.enter_context(nc.Block())


        def heads(i, t):
            return H_PAIR * i + t - HEADS

        def fills(i, g):
            return FILLS * i + g - FILLS // 2

        def stack_count(i, g):
            return STACK_INC * (FILLS // 2 * (i - 1) + g // 2 + 1)

        def direct(i, g):
            return isinstance(i, int) and i == 0 and g < FILLS

        def split_into(i, g):
            return stacks[:, g % 2, 0:2].rearrange("p h q n -> p (h q) n") if direct(i, g) else split[:]

        def batch(i, b):
            return 2 * i + b - 1

        def tokens(i, tile):
            return T_PAIR * i + tile - T_PAIR // 2

        def none(count):
            return isinstance(count, int) and count <= 0

        def sums(i, k, tile, step):
            before = 0 if isinstance(i, int) and i == 1 else groups * (T_PAIR * (i - 1) - T_PAIR // 2)
            return before + len(step.fed) * k + tile - step.fed[0]

        def row(array, i):
            if isinstance(i, int):
                return array[i]
            names = "abcd"[:len(array.shape) - 1]
            return array[bass.ds(i, 1)].rearrange(f"z {' '.join(names)} -> (z a) {' '.join(names[1:])}")

        def fill_at(t, step):
            if t % 4 == 0 and t in step.heads and t // 4 + 1 <= (3 if step is LAST_HEADS else FILLS):
                return t // 4 + 1

        def fill_use(i, g):
            return g - FILLS // 2 if isinstance(i, int) and i == 0 else USES * i + g - USES // 2

        def y_use(i, tile, step):
            return fill_use(i, 4 if step is LAST_HEADS else FILLS + 1) + tile - step.y_tiles[0]

        def last_y_split(i):
            if isinstance(i, int) and i == pairs + 1:
                return y_use(pairs, 1, LAST_HEADS) + 1
            return fill_use(i, 1)

        def y_split_at(t, part, step):
            tile = (Y_SPLIT_SECOND if step is SECOND else Y_SPLIT).get((t, part))
            return tile if tile in step.y_tiles else None

        def down_bank(a, tile, step):
            n = tile - step.fed[0]
            if a == groups - 1 and n >= 2:
                return (up_ps, down_ps[0])[n - 2]
            return down_ps[n % 2]

        def gates_ended(t, part, step):
            before = (t, part - 1) if part else (t - 1, 2)
            return [a for kind, a, _ in ends[step.fed].get(before, []) if kind == "gate"]

        def fed_x(step):
            return x_att if step is LAST else x_ffn

        def columns(step):
            return slice(P * step.fed[0], P * (step.fed[-1] + 1))

        pieces = h_tiles + groups
        w_buffers = [gu_raw[:].rearrange("p u k n -> p (u k n)")] + [
            b.rearrange("p t d -> p (t d)") for b in (dn_raw[:], x_ffn[:, 0:2], x_ffn[:, 2:4], h_full[:], x_att[:, 0:2])]
        assert len(w_buffers) == W_BUFFERS

        def pieces_at(t):
            return [n for n in range(pieces) if t == FIRST.heads[0] + 2 * n // 3]

        def raw_gu(i, j, step):
            if step in (SECOND, LAST):
                if j % 2 == 1:
                    spare = x_ffn[:, 0:2] if step is SECOND else x_in[:]
                    return (spare.rearrange("p t d -> p (t d)"), gu_spare_loaded,
                            16 * ((0 if step is SECOND else h_tiles // 2) + j // 2 + 1))
                count = (0 if step is SECOND else h_tiles // 2 + h_tiles * (i - 2)) + j // 2 + 1
            else:
                count = h_tiles // 2 + h_tiles * (i - 2) + j + 1
            return gu_raw[:].rearrange("p u k n -> p (u k n)"), gu_loaded, 16 * count

        def later(i, j, step):
            if j < h_tiles:
                return i, j, step
            return i + 1, j - h_tiles, {FIRST: SECOND, SECOND: MIDDLE, MIDDLE: MIDDLE, LAST_HEADS: LAST}[step]

        def hi_weights(n):
            if n < h_tiles:
                return gu_hi[:, n].rearrange("p u k n -> p (u k n)")
            return dn_hi[:, per * (n - h_tiles):per * (n - h_tiles + 1)].rearrange("p h d -> p (h d)")

        @block.sync
        def _(sp):
            def load_batch(i, b):
                n = batch(i, b)
                if not none(n):
                    sp.wait_ge(turned, fill_use(i, 4 * b))
                    sp.sem_inc(sp_passed, 1)
                    sp.wait_ge(v_ready, 2 * n)
                    sp.sem_inc(sp_passed, 1)
                sp.dma_start(x_in[:], row(x_batch, n)).then_inc(x_in_loaded, 16)
                sp.dma_start(ctx_in[:], row(ctx_batch, n)).then_inc(ctx_loaded, 16)

            def fill_stack(i, g):
                sp.wait_ge(turn_lo_done, fill_use(i, g) + 1)
                sp.sem_inc(sp_passed, 1)
                if not none(fills(i, g - 1)):
                    sp.wait_ge(scores_done, heads(i, 4 * (g - 1)))
                for j in range(4):
                    for r, parts in enumerate((slice(0, 3, 2), slice(0, 4, 3), slice(1, 3, 1))):
                        sp.dma_start(stacks[HD * r:HD * r + HD, g % 2, j, :, :].bitcast(F32),
                                     split[HD * j:HD * j + HD, parts, :].bitcast(F32)).then_inc(stack_loaded[g % 2][j], 16)

            def load_gu(i, j, step):
                i, j, step = later(i, j, step)
                buffer, loaded, _ = raw_gu(i, j, step)
                sp.dma_start(buffer, gu_w[j].rearrange("p u k n -> p (u k n)")).then_inc(loaded, 16)

            def load_dn(k):
                sp.dma_start(dn_raw[:], dn_w[k]).then_inc(dn_loaded, 16)

            def hand_over(i, tiles):
                sp.wait_ge(y_normed, tokens(i - 1, tiles[-1]) + 1)
                sp.dma_start(x_ffn[:, tiles[0]:tiles[-1] + 1], x_att[:, tiles[0]:tiles[-1] + 1]).then_inc(x_ffn_loaded, 16)

            def load_x(i, step):
                if not none(i):
                    sp.wait_ge(x_ffn_loaded, 16 * i)
                    sp.sem_inc(sp_passed, 1)
                tiles = slice(step.y_tiles[0], step.y_tiles[-1] + 1)
                if len(step.y_tiles) == 2:
                    source = x_batch[0 if step is FIRST else batches - 1]
                else:
                    source = row(x_pair, i - 1)
                sp.dma_start(x_att[:, tiles], source).then_inc(x_att_loaded, 16)

            def attention(i, t, step):
                if t == 8 and step.batches >= 1:
                    load_batch(i, 1)
                if t == 24 and step.batches == 2:
                    load_batch(i, 2)
                if fill_at(t, step) is not None and not direct(i, fill_at(t, step)):
                    fill_stack(i, fill_at(t, step))

            def feed_forward(i, t, step):
                for part in range(3):
                    for kind, a, b in ends[step.fed].get((t, part), []):
                        if kind == "up":
                            two = (step is LAST or (step is SECOND and a + 4 <= h_tiles)
                                   or (step is LAST_HEADS and a + 4 > h_tiles + 1))
                            j = a + (4 if two else 3)
                            if (step is LAST and j >= h_tiles) or (step is SECOND and a + 3 == h_tiles):
                                continue
                            sp.wait_ge(gu_lo_done, h_tiles * (i - 1) + a + 3)
                            load_gu(i, j, step)
                            if step is LAST_HEADS and a + 3 == h_tiles:
                                sp.wait_ge(turned, fill_use(i, 4))
                                load_gu(i, j + 1, step)
                        if kind == "down" and b == step.fed[-1] and not (step is LAST and a + 2 >= groups):
                            sp.wait_ge(dn_lo_done, groups * (i - 1) + a + 2)
                            load_dn((a + 2) % groups)

            def store(i, step):
                if len(step.fed) == 2:
                    target = out_batch[0 if step is SECOND else batches - 1]
                else:
                    target = row(out_pair, i - 2)
                for tile in step.fed:
                    sp.wait_ge(down_free, 2 + sums(i, groups - 1, tile, step) + 1)
                    sp.sem_inc(sp_passed, 1)
                    sp.dma_start(target[:, tile - step.fed[0], :], fed_x(step)[:, tile, :]).then_inc(out_stored, 16)
                sp.wait_ge(out_stored, 16 * (tokens(i - 1, step.fed[-1]) + 1))
                sp.sem_inc(sp_passed, 1)

            load_batch(0, 1)
            load_x(0, FIRST)
            for t in range(FIRST.heads[0], TICKS):
                attention(0, t, FIRST)
                if t == PIECES_READ:
                    sp.wait_ge(w_hi_done[0], pieces // 2)
                    sp.wait_ge(w_hi_done[1], pieces // 2)
                    load_gu(1, 0, SECOND)
                    load_dn(0)
                    load_gu(1, 1, SECOND)
            for n in range(2):
                sp.wait_ge(gu_lo_done, n + 1)
                load_gu(1, n + 2, SECOND)
            sp.wait_ge(dn_lo_done, 1)
            load_dn(1)

            def run(i, step, before):
                if step is not LAST:
                    hand_over(i, before.y_tiles)
                for t in range(TICKS):
                    if t == 2 and step is not LAST:
                        load_x(i, step)
                    attention(i, t, step)
                    feed_forward(i, t - 1, step)
                feed_forward(i, TICKS - 1, step)
                store(i, step)

            run(1, SECOND, FIRST)
            with sp.Fori(2, pairs) as i:
                run(i, MIDDLE, MIDDLE)
            run(pairs, LAST_HEADS, MIDDLE)
            run(pairs + 1, LAST, LAST_HEADS)

        @block.tensor
        def _(pe):
            def turn_qk(i, g):
                if g % 4 == 0:
                    pe.wait_ge(in_normed, 2 * batch(i, g // 4) + 2)
                    pe.wait_ge(ctx_loaded, 16 * batch(i, g // 4) + 16)
                if g == 1:
                    pe.wait_ge(turn_lo_done, fill_use(0, FILLS) + 1 if isinstance(i, int) and i == 1 else
                               y_use(i - 1, 0, MIDDLE) + 1)
                elif not none(fill_use(i, g)):
                    pe.wait_ge(turn_lo_done, fill_use(i, g))
                c = (g % 4) * P
                for n, source in enumerate((x_in, ctx_in)):
                    for tile in range(2):
                        mm = pe.transpose(turn_ps[:, (2 * n + tile) * P:(2 * n + tile + 1) * P],
                                          source[:, tile, c:c + P], ident[:])
                mm.then_inc(turned, 1)

            def scores(i, t):
                if direct(i, t // 4):
                    pe.wait_ge(turn_lo_done, fill_use(i, t // 4) + 1)
                else:
                    pe.wait_ge(stack_loaded[t // 4 % 2][t % 4], stack_count(i, t // 4))
                if not none(heads(i, t)):
                    pe.wait_ge(masked, 2 * heads(i, t))
                if t == 0 and not (isinstance(i, int) and i == 1):
                    pe.wait_ge(turn_lo_done, y_use(i - 1, 1, MIDDLE) + 1)
                if direct(i, t // 4):
                    s = split_into(i, t // 4)[HD * (t % 4):HD * (t % 4 + 1)]
                    for tile in range(2):
                        for n, (q, k) in enumerate(((0, 2), (0, 3), (1, 2))):
                            mm = pe.matmul(score_ps[:, tile * 2 * P:(tile + 1) * 2 * P],
                                           s[:, q, tile * P:(tile + 1) * P], s[:, k, :], start=n == 0, stop=n == 2)
                    mm.then_inc(scores_done, 1)
                    return
                s = stacks[0:3 * HD, t // 4 % 2, t % 4]
                for tile in range(2):
                    mm = pe.matmul(score_ps[:, tile * 2 * P:(tile + 1) * 2 * P],
                                   s[:, 0, tile * P:(tile + 1) * P], s[:, 1, :], start=True, stop=True)
                mm.then_inc(scores_done, 1)

            def turn_probs(i, t):
                pe.wait_ge(exp_done, 2 * heads(i, t) + 2)
                if not none(heads(i, t)):
                    pe.wait_ge(pt_lo_done, heads(i, t))
                for n in range(3):
                    mm = pe.transpose(pt_ps[:, n * P:(n + 1) * P], probs[:, t % 2, n * P:(n + 1) * P], ident[:])
                mm.then_inc(pt_done, 1)

            def values(i, t):
                if t % 8 == 0:
                    pe.wait_ge(v_ready, 2 * batch(i, 0) + t // 8 + 1)
                pe.wait_ge(pt_lo_done, heads(i, t) + 1)
                if not none(heads(i, t)):
                    pe.wait_ge(pv_reduced, heads(i, t))
                for tile, blocks in enumerate((((0, 0),), ((1, 0), (2, 1)))):
                    for n, (b, keys) in enumerate(blocks):
                        for part in (pt_hi, pt_lo):
                            mm = pe.matmul(pv_ps[:, tile * 3 * VP:(tile + 1) * 3 * VP],
                                           part[:, t % 2, b * P:(b + 1) * P],
                                           v_parts[:, keys, t % HEADS].rearrange("p a v -> p (a v)"),
                                           start=(n == 0 and part is pt_hi),
                                           stop=(n == len(blocks) - 1 and part is pt_lo))
                mm.then_inc(pv_done, 1)

            def turn_y(i, tile, step):
                pe.wait_ge(y_normed, tokens(i, tile) + 1)
                if tile == 0:
                    pe.wait_ge(turn_lo_done, y_use(i, tile, step))
                for k in range(kd):
                    mm = pe.transpose(y_ps[tile][:, k * P:(k + 1) * P],
                                      y_in[:, k * P:(k + 1) * P], ident[:])
                mm.then_inc(turned, 1)

            def product(i, n, step):
                kind, a, b, c = orders[step.fed][n]
                if kind == "down":
                    first = b == step.fed[0]
                    hh, term = divmod(c, 3)
                    term = (0, 2, 1)[term]
                    if c == 0:
                        if a == groups - 1 and b - step.fed[0] == 2:
                            pe.wait_ge(up_free, h_tiles * (i - 1) + h_tiles + 1)
                        else:
                            behind = {(groups - 1, 3): 3, (0, 0): 1}.get((a, b - step.fed[0]), 2)
                            pe.wait_ge(down_free, 2 + sums(i, a, b, step) - behind + 1)
                    if first and c == 0:
                        pe.wait_ge(dn_lo_done, groups * (i - 1) + a + 1)
                    if first and term == 0:
                        pe.wait_ge(h_hi_done, h_tiles * (i - 1) + per * a + hh + 1)
                    if first and term == 1:
                        pe.wait_ge(h_lo_done, 2 + h_tiles * (i - 1) + per * a + hh + 1)
                    mm = pe.matmul(down_bank(a, b, step)[:], (h_lo if term == 1 else h_hi)[:, hh, b * P:(b + 1) * P],
                                   dn_lo[:, hh] if term == 2 else dn_hi[:, per * a + hh],
                                   start=(c == 0), stop=(c == 3 * per - 1))
                    if c == 3 * per - 1:
                        mm.then_inc(down_done, 1)
                    return
                u = 0 if kind == "gate" else 1
                k, term = divmod(c, 3)
                if c == 0:
                    pe.wait_ge((gate_free, up_free)[u], h_tiles * (i - 1) + a + 1)
                if c == 0 and u == 1 and a == 0:
                    pe.wait_ge(down_free, sums(i, 0, step.fed[0], step) + 1)
                if c == 0 and u == 0:
                    pe.wait_ge(gu_lo_done, h_tiles * (i - 1) + a + 1)
                mm = pe.matmul((gate_ps, up_ps)[u][:, columns(step)],
                               gu_lo[:, a % 2, u, k] if term == 2 else gu_hi[:, a, u, k],
                               (yt_lo if term == 1 else yt_hi)[:, k, columns(step)], start=(c == 0), stop=(c == 3 * kd - 1))
                if c == 3 * kd - 1:
                    mm.then_inc((gate_done, up_done)[u], 1)

            def run(i, step):
                for t in range(FIRST.heads[0] if step is FIRST else 0, TICKS):
                    for part in range(3):
                        if part == 0 and t in step.heads:
                            scores(i, t)
                        if part == 0 and fill_at(t, step) is not None:
                            turn_qk(i, fill_at(t, step))
                        if part == 1 and t - LAG_T in step.heads:
                            turn_probs(i, t - LAG_T)
                        if part == 2 and t - LAG_V in step.heads:
                            values(i, t - LAG_V)
                        if Y_TURNED.get((t, part)) in step.y_tiles:
                            turn_y(i, Y_TURNED[t, part], step)
                        if step.fed and (t, part) == (0, 0):
                            pe.wait_ge(turn_lo_done, last_y_split(i))
                        if step.fed:
                            for n in range(len(orders[step.fed])):
                                if part_of(step.fed, n) == (t, part):
                                    product(i, n, step)

            pe.wait_ge(consts_ready, 4)
            turn_qk(0, FIRST.heads[0] // 4)
            run(0, FIRST)
            pe.wait_ge(w_hi_done[0], pieces // 2)
            pe.wait_ge(w_hi_done[1], pieces // 2)
            run(1, SECOND)
            with pe.Fori(2, pairs) as i:
                run(i, MIDDLE)
            run(pairs, LAST_HEADS)
            run(pairs + 1, LAST)

        @block.vector
        def _(dve):
            def input_stats(i, b, tile):
                dve.wait_ge(x_in_loaded, 16 * batch(i, b) + 16)
                dve.bn_stats(in_stats[:, tile, :], x_in[:, tile, :]).then_inc(in_stats_done, 1)

            def input_moments(i, b):
                n = batch(i, b)
                dve.wait_ge(in_stats_done, 2 * n + 2)
                dve.sem_inc(dve_passed, 1)
                for tile in range(2):
                    dve.bn_aggr(in_moments[:, tile, :], in_stats[:, tile, :]).then_inc(in_moments_done, 1)
                dve.wait_ge(in_moments_done, 2 * n + 2)
                dve.tensor_scalar(in_var[:], in_moments[:, :, 1], EPS, None, ALU.add).then_inc(in_var_done, 1)

            def input_norm(i, b):
                dve.wait_ge(in_rstd_done, batch(i, b) + 1)
                for tile in range(2):
                    dve.tensor_scalar(x_in[:, tile, :], x_in[:, tile, :], in_moments[:, tile, 0:1],
                                      in_rstd[:, tile:tile + 1], ALU.subtract, ALU.mult).then_inc(in_normed, 1)

            def y_stats_of(i, tile):
                if tile % 2 == 0:
                    dve.wait_ge(x_att_added, fills(i, 2 * tile + 4))
                dve.bn_stats(y_stats[:, tile % 2, :], x_att[:, tile, :]).then_inc(y_stats_done, 1)

            def y_moments_of(i, half):
                dve.wait_ge(y_stats_done, tokens(i, 2 * half) + 2)
                dve.sem_inc(dve_passed, 1)
                for tile in range(2):
                    dve.bn_aggr(y_moments[:, 2 * half + tile, :], y_stats[:, tile, :]).then_inc(y_moments_done, 1)
                dve.wait_ge(y_moments_done, tokens(i, 2 * half) + 2)
                dve.tensor_scalar(y_var[:, 2 * half:2 * half + 2], y_moments[:, 2 * half:2 * half + 2, 1],
                                  EPS, None, ALU.add).then_inc(y_var_done, 1)

            def y_norm(i, tile, step):
                if tile % 2 == 0:
                    dve.wait_ge(y_rstd_done, batch(i, tile // 2) + 1)
                if tile != step.y_tiles[0]:
                    dve.wait_ge(turned, y_use(i, tile, step))
                dve.tensor_scalar(y_in[:], x_att[:, tile, :], y_moments[:, tile, 0:1],
                                  y_rstd[:, tile:tile + 1], ALU.subtract, ALU.mult).then_inc(y_normed, 1)

            def mask_scores(i, t):
                dve.wait_ge(scores_done, heads(i, t) + 1)
                if not none(heads(i, t) - 1):
                    dve.wait_ge(pt_done, heads(i, t) - 1)
                dve.sem_inc(dve_passed, 1)
                for tile, (lo, hi, m) in enumerate(((0, P, P), (P, 3 * P, 0))):
                    dve.tensor_tensor_reduce(probs[:, t % 2, lo:hi], score_ps[:, tile * 2 * P:tile * 2 * P + hi - lo],
                                             mask[:, m:], -SCALE, -NEG, ALU.add, ALU.min,
                                             neg_max[:, t % 2, tile:tile + 1]).then_inc(masked, 1)

            def split_qk_lo(i, g):
                use = fill_use(i, g)
                dve.wait_ge(turn_hi_done, use + 1)
                parts = split_into(i, g)
                dve.tensor_tensor(parts[:, 1:4:2, :], turn_ps[:].rearrange("p (a n) -> p a n", a=2),
                                  parts[:, 0:4:2, :].bitcast(F32), ALU.subtract).then_inc(turn_lo_done, 1)

            def split_y_lo(i, tile, step):
                dve.wait_ge(turn_hi_done, y_use(i, tile, step) + 1)
                cols = slice(tile * P, (tile + 1) * P)
                dve.tensor_tensor(yt_lo[:, :, cols], y_ps[tile][:].rearrange("p (k n) -> p k n", k=kd),
                                  yt_hi[:, :, cols].bitcast(F32), ALU.subtract).then_inc(turn_lo_done, 1)

            def split_probs_lo(i, t):
                dve.wait_ge(pt_hi_done, heads(i, t) + 1)
                dve.scalar_tensor_tensor(out=pt_lo[:, t % 2, :], in0=pt_ps[:, 0:3 * P], scalar=P_SCALE,
                                         in1=pt_hi[:, t % 2, :], op0=ALU.mult, op1=ALU.subtract
                                         ).then_inc(pt_lo_done, 1)

            def collect_head(i, t):
                dve.wait_ge(pv_done, heads(i, t) + 1)
                if t % 4 == 0 and not none(heads(i, t)):
                    dve.wait_ge(x_att_added, fills(i, t // 4))
                dve.tensor_reduce(heads_out[:, :, t % 4, :],
                                  pv_ps[:, 0:6 * VP].rearrange("p (q a v) -> p q v a", q=2, a=3),
                                  AX.X, ALU.add).then_inc(pv_reduced, 1)
                if t % 4 < 3:
                    return
                g = t // 4
                dve.wait_ge(pv_reduced, heads(i, t) + 1)
                dve.reciprocal(quotient[:], heads_out[:, :, :, HD]).then_inc(quotient_done, 1)
                dve.wait_ge(quotient_done, fills(i, g) + 1)
                dve.tensor_tensor(heads_out[:, :, :, 0:HD], heads_out[:, :, :, 0:HD],
                                  quotient[:].unsqueeze(3).broadcast_to([P, 2, 4, HD]), ALU.mult
                                  ).then_inc(heads_scaled, 1)
                if g == 0 or none(fills(i, g)):
                    dve.wait_ge(x_att_loaded, 16 * i + 16)
                dve.wait_ge(heads_scaled, fills(i, g) + 1)
                xs = x_att[:, 2 * (g // 4):2 * (g // 4) + 2, (g % 4) * P:(g % 4 + 1) * P].rearrange(
                    "p q (h d) -> p q h d", h=4)
                dve.tensor_tensor(xs, xs, heads_out[:, :, :, 0:HD], ALU.add).then_inc(x_att_added, 1)

            def gated(i, j, step):
                n = h_tiles * (i - 1) + j
                dve.wait_ge(tanh_done, n + 1)
                hf = h_full[:, j % 2, columns(step)]
                dve.scalar_tensor_tensor(out=hf, in0=hf, scalar=1.0, in1=gate_ps[:, columns(step)], op0=ALU.add, op1=ALU.mult
                                         ).then_inc(gate_free, 1)

            def hidden(i, j, step):
                n = h_tiles * (i - 1) + j
                dve.wait_ge(up_done, n + 1)
                dve.wait_ge(gate_free, n + 2)
                hf = h_full[:, j % 2, columns(step)]
                dve.scalar_tensor_tensor(out=hf, in0=hf, scalar=0.5, in1=up_ps[:, columns(step)], op0=ALU.mult, op1=ALU.mult
                                         ).then_inc(up_free, 1)

            def add_down(i, k, tile, step):
                n = sums(i, k, tile, step)
                dve.wait_ge(down_done, n + 1)
                if k == 0 and tile == step.fed[0] and step is not LAST:
                    dve.wait_ge(x_ffn_loaded, 16 * i)
                if k:
                    dve.wait_ge(down_free, 2 + n - len(step.fed) + 1)
                x = fed_x(step)[:, tile, :]
                dve.tensor_tensor(x, x, down_bank(k, tile, step)[:], ALU.add
                                  ).then_inc(down_free, 1)

            def weights_gu_lo(i, j, step):
                raw, loaded, count = raw_gu(i, j, step)
                dve.wait_ge(gu_lo_done, h_tiles * (i - 1) + j)
                dve.wait_ge(loaded, count)
                dve.tensor_tensor(gu_lo[:, j % 2].rearrange("p u k n -> p (u k n)"), raw,
                                  gu_hi[:, j].bitcast(F32).rearrange("p u k n -> p (u k n)"), ALU.subtract
                                  ).then_inc(gu_lo_done, 1)

            def weights_hi(n):
                dve.wait_ge(w_loaded[n % W_BUFFERS], 16 * (n // W_BUFFERS) + 16)
                dve.tensor_copy(hi_weights(n), w_buffers[n % W_BUFFERS]).then_inc(w_hi_done[1], 1)

            def run(i, step):
                for t in range(FIRST.heads[0] if step is FIRST else 0, TICKS):
                    for part in range(3):
                        if step is FIRST and part == 2:
                            for n in pieces_at(t):
                                if n % 2 == 1:
                                    weights_hi(n)
                        if part == 0 and t in step.heads:
                            mask_scores(i, t)
                        if part == 1 and fill_at(t, step) is not None:
                            split_qk_lo(i, fill_at(t, step))
                        if part == (2 if step.fed else 1) and t - LAG_T in step.heads:
                            split_probs_lo(i, t - LAG_T)
                        for j in gates_ended(t, part, step):
                            gated(i, j, step)
                        if part == 2 and t - LAG_V in step.heads:
                            collect_head(i, t - LAG_V)
                        if (t, part) in INPUT_STATS and INPUT_STATS[t, part][0] <= step.batches:
                            input_stats(i, *INPUT_STATS[t, part])
                        if INPUT_MOMENTS.get((t, part), 3) <= step.batches:
                            input_moments(i, INPUT_MOMENTS[t, part])
                        if INPUT_NORM.get((t, part), 3) <= step.batches:
                            input_norm(i, INPUT_NORM[t, part])
                        if Y_STATS.get((t, part)) in step.y_tiles:
                            y_stats_of(i, Y_STATS[t, part])
                        if (t, part) in Y_MOMENTS and 2 * Y_MOMENTS[t, part] in step.y_tiles:
                            y_moments_of(i, Y_MOMENTS[t, part])
                        if Y_NORM.get((t, part)) in step.y_tiles:
                            y_norm(i, Y_NORM[t, part], step)
                        for kind, a, b in ends[step.fed].get((t, part), []):
                            if kind == "up":
                                hidden(i, a, step)
                                if step is LAST and a + 2 < h_tiles:
                                    weights_gu_lo(i, a + 2, step)
                            if kind == "down":
                                add_down(i, a, b, step)
                            if step is MIDDLE and (kind, a, b) == ("down", groups - 1, 0):
                                split_y_lo(i, T_PAIR - 1, step)
                        tile = y_split_at(t, part, step)
                        if tile is not None and not (step is MIDDLE and tile == T_PAIR - 1):
                            split_y_lo(i, tile, step)

            dve.sem_inc(gate_free, 1)
            dve.sem_inc(up_free, 1)
            dve.sem_inc(down_free, 2)
            for tile in range(2):
                input_stats(0, 1, tile)
            input_moments(0, 1)
            input_norm(0, 1)
            dve.wait_ge(consts_ready, 3)
            split_qk_lo(0, FIRST.heads[0] // 4)
            run(0, FIRST)
            run(1, SECOND)
            with dve.Fori(2, pairs) as i:
                run(i, MIDDLE)
            run(pairs, LAST_HEADS)
            run(pairs + 1, LAST)

        @block.scalar
        def _(act):
            def load_piece(n):
                if n >= W_BUFFERS:
                    act.wait_ge(w_hi_done[n % 2], (n - W_BUFFERS) // 2 + 1)
                source = (gu_w[n].rearrange("p u k n -> p (u k n)") if n < h_tiles else
                          dn_w[n - h_tiles].rearrange("p h d -> p (h d)"))
                act.dma_start(w_buffers[n % W_BUFFERS], source).then_inc(w_loaded[n % W_BUFFERS], 16)

            def exponentials(i, t):
                for tile, (lo, hi) in enumerate(((0, P), (P, 3 * P))):
                    act.wait_ge(masked, 2 * heads(i, t) + tile + 1)
                    p = probs[:, t % 2, lo:hi]
                    act.activation(p, p, ACT.Exp, bias=neg_max[:, t % 2, tile:tile + 1], scale=-1.0
                                   ).then_inc(exp_done, 1)

            def split_qk_hi(i, g):
                act.wait_ge(turned, fill_use(i, g) + 1)
                if direct(i, g):
                    if g >= FIRST.heads[0] // 4 + 2:
                        act.wait_ge(scores_done, heads(i, 4 * (g - 1)))
                elif not direct(i, g - 1):
                    for j in range(4):
                        act.wait_ge(stack_loaded[(g - 1) % 2][j], stack_count(i, g - 1))
                act.activation(split_into(i, g)[:, 0:4:2, :], turn_ps[:].rearrange("p (a n) -> p a n", a=2), ACT.Copy
                               ).then_inc(turn_hi_done, 1)

            def split_y_hi(i, tile, step):
                act.wait_ge(turned, y_use(i, tile, step) + 1)
                if step.fed and tile == step.fed[0]:
                    act.wait_ge(up_done, h_tiles * i)
                act.activation(yt_hi[:, :, tile * P:(tile + 1) * P],
                               y_ps[tile][:].rearrange("p (k n) -> p k n", k=kd), ACT.Copy
                               ).then_inc(turn_hi_done, 1)

            def split_probs_hi(i, t):
                act.wait_ge(pt_done, heads(i, t) + 1)
                if not none(heads(i, t) - 1):
                    act.wait_ge(pv_done, heads(i, t) - 1)
                act.activation(pt_hi[:, t % 2, :], pt_ps[:, 0:3 * P], ACT.Copy, scale=P_SCALE
                               ).then_inc(pt_hi_done, 1)

            def values_first(i, b, half):
                n = batch(i, b)
                act.wait_ge(ctx_loaded, 16 * n + 16)
                if not none(n):
                    act.wait_ge(pv_done, HEADS * n - HEADS // 2 + 8 * half)
                h = slice(8 * half, 8 * half + 8)
                act.activation(v_parts[:, :, h, 0, 0:HD],
                               ctx_in[:].rearrange("p t (h d) -> p t h d", h=HEADS)[:, :, h, :], ACT.Copy
                               ).then_inc(v1_done, 1)

            def values_second(i, b, half):
                act.wait_ge(v_rest_done, 2 * batch(i, b) + half + 1)
                act.activation(v_parts[:, :, 8 * half:8 * half + 8, 1, 0:HD], v_rest[:], ACT.Copy
                               ).then_inc(v2_done, 1)

            def tanh(i, j, step):
                n = h_tiles * (i - 1) + j
                act.wait_ge(gate_done, n + 1)
                act.wait_ge(h_lo_done, n + 1)
                act.activation(h_full[:, j % 2, columns(step)], gate_ps[:, columns(step)], ACT.Tanh, scale=0.5).then_inc(tanh_done, 1)

            def split_h_hi(i, j, step):
                act.wait_ge(up_free, h_tiles * (i - 1) + j + 2)
                act.activation(h_hi[:, j % per, columns(step)], h_full[:, j % 2, columns(step)], ACT.Copy).then_inc(h_hi_done, 1)

            def weights_hi(n):
                act.wait_ge(w_loaded[n % W_BUFFERS], 16 * (n // W_BUFFERS) + 16)
                act.activation(hi_weights(n), w_buffers[n % W_BUFFERS], ACT.Copy).then_inc(w_hi_done[0], 1)

            def run(i, step):
                for t in range(FIRST.heads[0] if step is FIRST else 0, TICKS):
                    for part in range(3):
                        if part == 0 and fill_at(t, step) is not None:
                            split_qk_hi(i, fill_at(t, step))
                        if part == 1 and t - LAG_T in step.heads:
                            split_probs_hi(i, t - LAG_T)
                        if part == 1 and t in step.heads:
                            exponentials(i, t)
                        if (t, part) in VALUES_1 and VALUES_1[t, part][0] <= step.batches:
                            values_first(i, *VALUES_1[t, part])
                        if (t, part) in VALUES_2 and VALUES_2[t, part][0] <= step.batches:
                            values_second(i, *VALUES_2[t, part])
                        if y_split_at(t, part, step) is not None:
                            split_y_hi(i, y_split_at(t, part, step), step)
                        for kind, a, b in ends[step.fed].get((t, part), []):
                            if kind == "gate":
                                tanh(i, a, step)
                            if kind == "up":
                                split_h_hi(i, a, step)
                        if step is FIRST and part == 2:
                            for n in pieces_at(t):
                                if n % 2 == 0:
                                    weights_hi(n)
                            for n in pieces_at(t - 1):
                                if n + W_BUFFERS < pieces:
                                    load_piece(n + W_BUFFERS)

            values_first(0, 1, 0)
            for n in range(W_BUFFERS):
                load_piece(n)
            split_qk_hi(0, FIRST.heads[0] // 4)
            values_second(0, 1, 0)
            run(0, FIRST)
            run(1, SECOND)
            with act.Fori(2, pairs) as i:
                run(i, MIDDLE)
            run(pairs, LAST_HEADS)
            run(pairs + 1, LAST)

        @block.gpsimd
        def _(pool):
            def input_rstd(i, b):
                pool.wait_ge(in_var_done, batch(i, b) + 1)
                pool.tensor_tensor(in_rstd[:], in_var[:], minus_half[:], ALU.pow).then_inc(in_rstd_done, 1)

            def y_rstd_of(i, half):
                pool.wait_ge(y_var_done, batch(i, half) + 1)
                tiles = slice(2 * half, 2 * half + 2)
                pool.tensor_tensor(y_rstd[:, tiles], y_var[:, tiles], minus_half[:], ALU.pow).then_inc(y_rstd_done, 1)

            def values_rest(i, b, half):
                h = slice(8 * half, 8 * half + 8)
                pool.wait_ge(v1_done, 2 * batch(i, b) + half + 1)
                if not none(2 * batch(i, b) + half):
                    pool.wait_ge(v_ready, 2 * batch(i, b) + half)
                pool.tensor_tensor(v_rest[:], ctx_in[:].rearrange("p t (h d) -> p t h d", h=HEADS)[:, :, h, :],
                                   v_parts[:, :, h, 0, 0:HD], ALU.subtract).then_inc(v_rest_done, 1)

            def values_third(i, b, half):
                pool.wait_ge(v2_done, 2 * batch(i, b) + half + 1)
                h = slice(8 * half, 8 * half + 8)
                pool.tensor_tensor(v_parts[:, :, h, 2, 0:HD], v_rest[:], v_parts[:, :, h, 1, 0:HD],
                                   ALU.subtract).then_inc(v_ready, 1)

            def split_h_lo(i, j, step):
                pool.wait_ge(h_hi_done, h_tiles * (i - 1) + j + 1)
                pool.tensor_tensor(h_lo[:, j % per, columns(step)], h_full[:, j % 2, columns(step)],
                                   h_hi[:, j % per, columns(step)].bitcast(F32), ALU.subtract).then_inc(h_lo_done, 1)

            def weights_gu_lo(i, j, step):
                i, j, step = later(i, j, step)
                raw, loaded, count = raw_gu(i, j, step)
                pool.wait_ge(loaded, count)
                pool.tensor_tensor(gu_lo[:, j % 2].rearrange("p u k n -> p (u k n)"), raw,
                                   gu_hi[:, j].bitcast(F32).rearrange("p u k n -> p (u k n)"), ALU.subtract
                                   ).then_inc(gu_lo_done, 1)

            def weights_dn_lo(n, k):
                pool.wait_ge(dn_loaded, 16 * (n + 1))
                pool.tensor_tensor(dn_lo[:], dn_raw[:], dn_hi[:, per * k:per * (k + 1)].bitcast(F32), ALU.subtract
                                   ).then_inc(dn_lo_done, 1)

            def run(i, step):
                for t in range(FIRST.heads[0] if step is FIRST else 0, TICKS):
                    for part in range(3):
                        if (t, part) in VALUES_1 and VALUES_1[t, part][0] <= step.batches:
                            values_rest(i, *VALUES_1[t, part])
                        if (t, part) in VALUES_3 and VALUES_3[t, part][0] <= step.batches:
                            values_third(i, *VALUES_3[t, part])
                        if INPUT_RSTD.get((t, part), 3) <= step.batches:
                            input_rstd(i, INPUT_RSTD[t, part])
                        if (t, part) in Y_RSTD and 2 * Y_RSTD[t, part] in step.y_tiles:
                            y_rstd_of(i, Y_RSTD[t, part])
                        for kind, a, b in ends[step.fed].get((t, part), []):
                            if kind == "up":
                                split_h_lo(i, a, step)
                                if step is not LAST:
                                    pool.wait_ge(up_done, h_tiles * (i - 1) + a + 1)
                                    weights_gu_lo(i, a + 2, step)
                            if kind == "down" and b == step.fed[-1] and (step is not LAST or a + 1 < groups):
                                pool.wait_ge(down_done, sums(i, a, b, step) + 1)
                                weights_dn_lo(groups * (i - 1) + a + 1, (a + 1) % groups)
                        if step is FIRST and (t, part) == LO_MADE:
                            pool.wait_ge(w_hi_done[0], pieces // 2)
                            pool.wait_ge(w_hi_done[1], pieces // 2)
                            weights_gu_lo(1, 0, SECOND)
                            weights_gu_lo(1, 1, SECOND)
                            weights_dn_lo(0, 0)

            pool.sem_inc(h_lo_done, 2)
            pool.memset(minus_half[:], -0.5)
            pool.memset(ident[:], 0.0).then_inc(zeroed, 1)
            pool.memset(mask[:], 0.0).then_inc(zeroed, 1)
            pool.wait_ge(zeroed, 2)
            pool.affine_select(out=ident[:], in_=ident[:], compare_op=ALU.not_equal, fill=1.0, base=0,
                               pattern=[[-1, P]], channel_multiplier=1).then_inc(consts_ready, 1)
            pool.affine_select(out=mask[:, P:], in_=mask[:, P:], compare_op=ALU.is_ge, fill=NEG, base=0,
                               pattern=[[-1, P]], channel_multiplier=1).then_inc(consts_ready, 1)
            pool.memset(v_parts[:, :, :, 0, HD], 1.0).then_inc(consts_ready, 1)
            input_rstd(0, 1)
            values_rest(0, 1, 0)
            pool.memset(v_parts[:, :, :, 1:3, HD], 0.0).then_inc(consts_ready, 1)
            values_third(0, 1, 0)
            run(0, FIRST)
            run(1, SECOND)
            with pool.Fori(2, pairs) as i:
                run(i, MIDDLE)
            run(pairs, LAST_HEADS)
            run(pairs + 1, LAST)


def kernel(x, ctx_2048, L0_ffn_w_gate, L0_ffn_w_up, L0_ffn_w_down):
    import numpy as np
    import concourse.bacc as bacc
    from concourse.bass_utils import run_bass_kernel_spmd

    x, ctx = np.ascontiguousarray(x), np.ascontiguousarray(ctx_2048)
    hidden, dim = L0_ffn_w_gate.shape
    h_tiles, kd = hidden // P, dim // P
    gu = np.stack([np.asarray(w).reshape(h_tiles, P, kd, P) for w in (L0_ffn_w_gate, L0_ffn_w_up)])
    gu = np.ascontiguousarray(gu.transpose(1, 4, 0, 3, 2))
    dn = np.ascontiguousarray(np.asarray(L0_ffn_w_down).reshape(dim, h_tiles // 2, 2, P).transpose(1, 3, 2, 0))

    nc = bacc.Bacc("TRN2", target_bir_lowering=False, num_devices=1)
    arrays = {"x_dram": x, "ctx_dram": ctx, "gu_dram": gu, "dn_dram": dn}
    args = [nc.dram_tensor(n, a.shape, mybir.dt.from_np(a.dtype), kind="ExternalInput").ap()
            for n, a in arrays.items()]
    out = nc.dram_tensor("out_dram", x.shape, F32, kind="ExternalOutput").ap()
    build(nc, *args, out)
    r = run_bass_kernel_spmd(nc, [arrays], core_ids=[0])
    return r.results[0]["out_dram"]
```
